# Optimizing a Trainium2 kernel written in Bass

```python
import numpy as np
import jax
import jax.numpy as jnp

def _softmax(x, axis=-1):
    return jax.nn.softmax(x, axis=axis)

def _gelu(x):
    return jax.nn.gelu(x, approximate=True)

def _silu(x):
    return jax.nn.silu(x)

def _sigmoid(x):
    return jax.nn.sigmoid(x)

def _layernorm(x, axis=-1, eps=1e-05):
    m = jnp.mean(x, axis=axis, keepdims=True)
    v = jnp.var(x, axis=axis, keepdims=True)
    return (x - m) / jnp.sqrt(v + eps)

def _scatter_add(tgt, idx, src, axis=0):
    return tgt.at[idx].add(src)

def _segment_sum(src, seg, n):
    return jax.ops.segment_sum(src, seg, n)
kernel_name = 'mk_prb_d1_jaxref_r8_2c0a81'

def setup_inputs(seed: int=0):
    np.random.seed(seed)
    _w = jnp.asarray

    def _L0_attn_setup():
        import jax, jax.numpy as jnp
        import numpy as np
        B, L, DIM = (4, 512, 128)
        H, DQK, DV, DINNER, CHUNK = (16, 64, 64, 64, 64)
        BASE_LR, BASE_WD = (0.001, 0.9)
        key = jax.random.key(seed)
        ks = jax.random.split(key, 9)

        def s(k, shape, scale):
            return jax.random.normal(k, shape, jnp.float32) * scale
        return {'x': jax.random.normal(ks[0], (B, L, DIM), jnp.float32), 'Wq': s(ks[1], (H * DQK, DIM), DIM ** (-0.5)), 'Wk': s(ks[2], (H * DQK, DIM), DIM ** (-0.5)), 'Wv': s(ks[3], (H * DV, DIM), DIM ** (-0.5)), 'Wlr': s(ks[4], (2 * H, DIM), DIM ** (-0.5)), 'Wbeta': s(ks[5], (2 * H, DIM), DIM ** (-0.5)), 'Wo': s(ks[6], (DIM, H * DV), (H * DV) ** (-0.5)), 'W_in_init': s(ks[7], (1, DINNER, H, DQK), DQK ** (-0.5)), 'W_out_init': s(ks[8], (1, DINNER, H, DV), DINNER ** (-0.5))}
    _L0_attn_in = _L0_attn_setup()

    def _L0_ffn_setup():
        import jax, jax.numpy as jnp
        import numpy as np
        TOP_P = 0.8
        B, T, H, F, E = (2, 256, 128, 512, 8)
        key = jax.random.key(seed)
        k0, k1, k2, k3 = jax.random.split(key, 4)
        x = jax.random.normal(k0, (B, T, H), jnp.float32)
        Wr = jax.random.normal(k1, (H, E), jnp.float32) * 0.02
        br = jnp.zeros((E,), jnp.float32)
        W1 = jax.random.normal(k2, (E, H, F), jnp.float32) * 0.02
        b1 = jnp.zeros((E, F), jnp.float32)
        W2 = jax.random.normal(k3, (E, F, H), jnp.float32) * 0.02
        b2 = jnp.zeros((E, H), jnp.float32)
        return {'x': x, 'Wr': Wr, 'br': br, 'W1': W1, 'b1': b1, 'W2': W2, 'b2': b2}
    _L0_ffn_in = _L0_ffn_setup()
    _d = {'L0_attn_x': _L0_attn_in['x'], 'L0_attn_Wq': _L0_attn_in['Wq'], 'L0_attn_Wk': _L0_attn_in['Wk'], 'L0_attn_Wv': _L0_attn_in['Wv'], 'L0_attn_Wlr': _L0_attn_in['Wlr'], 'L0_attn_Wbeta': _L0_attn_in['Wbeta'], 'L0_attn_Wo': _L0_attn_in['Wo'], 'L0_attn_W_in_init': _L0_attn_in['W_in_init'], 'L0_attn_W_out_init': _L0_attn_in['W_out_init'], 'L0_ffn_Wr': _L0_ffn_in['Wr'], 'L0_ffn_br': _L0_ffn_in['br'], 'L0_ffn_W1': _L0_ffn_in['W1'], 'L0_ffn_b1': _L0_ffn_in['b1'], 'L0_ffn_W2': _L0_ffn_in['W2'], 'L0_ffn_b2': _L0_ffn_in['b2']}
    _x0 = _d['L0_attn_x']
    _d['L0_attn_x'] = jax.random.normal(jax.random.fold_in(jax.random.key(seed), 1), (8, 1024, 128), dtype=_x0.dtype)
    del _x0
    return _d

def reference(L0_attn_x, L0_attn_Wq, L0_attn_Wk, L0_attn_Wv, L0_attn_Wlr, L0_attn_Wbeta, L0_attn_Wo, L0_attn_W_in_init, L0_attn_W_out_init, L0_ffn_Wr, L0_ffn_br, L0_ffn_W1, L0_ffn_b1, L0_ffn_W2, L0_ffn_b2):

    def _L0_attn_ref(x, Wq, Wk, Wv, Wlr, Wbeta, Wo, W_in_init, W_out_init):
        import jax, jax.numpy as jnp
        import numpy as np
        B, L, DIM = (4, 512, 128)
        H, DQK, DV, DINNER, CHUNK = (16, 64, 64, 64, 64)
        BASE_LR, BASE_WD = (0.001, 0.9)
        b, l, _ = x.shape
        nc = l // CHUNK
        q = jax.nn.silu(x @ Wq.T).reshape(b, l, H, DQK)
        k = jax.nn.silu(x @ Wk.T).reshape(b, l, H, DQK)
        v = (x @ Wv.T).reshape(b, l, H, DV)
        lr = jax.nn.sigmoid(x @ Wlr.T) * BASE_LR
        wd = jax.nn.sigmoid(x @ Wbeta.T) * BASE_WD

        def chunked(t):
            return jnp.moveaxis(t.reshape(b, nc, CHUNK, *t.shape[2:]), 1, 0)
        qc, kc, vc = (chunked(q), chunked(k), chunked(v))
        lr_c = chunked(lr).mean(axis=2)
        wd_c = chunked(wd).mean(axis=2)
        lr_in, lr_out = (lr_c[..., :H], lr_c[..., H:])
        wd_in, wd_out = (wd_c[..., :H], wd_c[..., H:])
        W_in0 = jnp.broadcast_to(W_in_init, (b, DINNER, H, DQK))
        W_out0 = jnp.broadcast_to(W_out_init, (b, DINNER, H, DV))

        def step(carry, xs):
            W_in, W_out = carry
            qi, ki, vi, li, lo, wi, wo = xs
            p_q = jax.nn.softmax(jnp.einsum('bnhd,bDhd->bnhD', qi, W_in), axis=1)
            o = jnp.einsum('bnhD,bDhd->bnhd', p_q, W_out)
            p = jax.nn.softmax(jnp.einsum('bnhd,bDhd->bnhD', ki, W_in), axis=1)
            grad_out = jnp.einsum('bnhD,bnhd->bDhd', -p, vi)
            a = jnp.einsum('bDhd,bnhd->bnhD', W_out, vi)
            s = jnp.sum(p * a, axis=-1, keepdims=True)
            g_z = -(p * a - p * s)
            grad_in = jnp.einsum('bnhd,bnhD->bDhd', ki, g_z)
            W_in = wi[:, None, :, None] * W_in - li[:, None, :, None] * grad_in
            W_out = wo[:, None, :, None] * W_out - lo[:, None, :, None] * grad_out
            return ((W_in, W_out), o)
        _, outs = jax.lax.scan(step, (W_in0, W_out0), (qc, kc, vc, lr_in, lr_out, wd_in, wd_out))
        o = jnp.moveaxis(outs, 0, 1).reshape(b, l, H * DV)
        return o @ Wo.T

    def _L0_ffn_ref(x, Wr, br, W1, b1, W2, b2):
        import jax, jax.numpy as jnp
        import numpy as np
        TOP_P = 0.8
        B, T, H, F, E = (2, 256, 128, 512, 8)
        probs = jax.nn.softmax(x @ Wr + br, axis=-1)
        sorted_idx = jnp.argsort(-probs, axis=-1)
        sorted_probs = jnp.take_along_axis(probs, sorted_idx, axis=-1)
        cum = jnp.cumsum(sorted_probs, axis=-1)
        mask = cum < TOP_P
        mask = mask.at[..., 0].set(True)
        inv = jnp.argsort(sorted_idx, axis=-1)
        keep = jnp.take_along_axis(mask, inv, axis=-1)
        gate = probs * keep
        h = jax.nn.relu(jnp.einsum('bth,ehf->betf', x, W1) + b1[None, :, None, :])
        y = jnp.einsum('betf,efh->beth', h, W2) + b2[None, :, None, :]
        return jnp.einsum('bte,beth->bth', gate, y)
    x = L0_attn_x
    xn = _layernorm(x, axis=-1)
    x = x + _L0_attn_ref(xn, L0_attn_Wq, L0_attn_Wk, L0_attn_Wv, L0_attn_Wlr, L0_attn_Wbeta, L0_attn_Wo, L0_attn_W_in_init, L0_attn_W_out_init) + _L0_ffn_ref(xn, L0_ffn_Wr, L0_ffn_br, L0_ffn_W1, L0_ffn_b1, L0_ffn_W2, L0_ffn_b2)
    return x

_drawn_inputs = setup_inputs


def setup_inputs(seed=0):
    import zlib

    import numpy as np

    out = dict(_drawn_inputs(seed))
    spreads = {'L0_ffn_br': (0.0, 0.382), 'L0_ffn_b1': (0.0, 0.8), 'L0_ffn_b2': (0.0, 0.267)}
    factors = {'L0_attn_Wq': 8.0,
     'L0_attn_Wk': 8.0,
     'L0_attn_Wv': 8.0,
     'L0_attn_Wlr': 8.0,
     'L0_attn_Wbeta': 8.0,
     'L0_attn_Wo': 8.0,
     'L0_attn_W_in_init': 8.0,
     'L0_attn_W_out_init': 8.0,
     'L0_ffn_W1': 2.801,
     'L0_ffn_Wr': 2.851}
    for name, (base, spread) in spreads.items():
        noise = np.random.default_rng([zlib.crc32(name.encode()), seed]).standard_normal(out[name].shape)
        drawn = base * np.exp(spread * noise) if base else spread * noise
        out[name] = jnp.asarray(drawn.astype(out[name].dtype))
    for name, factor in factors.items():
        out[name] = (out[name] * factor).astype(out[name].dtype)
    return out
```

```python
import concourse.bass as bass
from concourse import mybir
from concourse.alu_op_type import AluOpType as ALU
from contextlib import ExitStack

F32 = mybir.dt.float32
ACT = mybir.ActivationFunctionType
AX = mybir.AxisListType

P = 128
CHUNK = 64
SLOTS = 16
LEAD = 8
BASE_LR, BASE_WD = 0.001, 0.9
TOP_P = 0.8
LN_EPS = 1e-5


def build(nc, x, wqT, wkT, wvT, wlbT, woT, winT0, wout0, woutT0, wr, br, w1, b1T, w2, b2,
          ident, sel_half, sel_wd, sel_lr, tri, out):
    B, L, D = x.shape
    HD = wqT.shape[1]
    PAIRS = HD // P
    E, _, F = w1.shape
    FT = F // P
    CHUNKS = L // CHUNK
    BG = 4
    GROUPS = B // BG
    TW = 2
    TOK = BG * CHUNK
    STEPS = GROUPS * CHUNKS
    LR_ROWS = wlbT.shape[1]
    assert D == P and PAIRS * TW == SLOTS and E * 2 == SLOTS and FT == 4

    ctx = ExitStack()
    with ctx:
        def sb(name, shape):
            return ctx.enter_context(nc.sbuf_tensor(name, shape, F32))

        def bank(name):
            return ctx.enter_context(nc.psum_tensor(name, [P, 512], F32))

        def sem(name):
            return ctx.enter_context(nc.semaphore(name))

        wq_s = sb("wq_s", [P, HD])
        wk_s = sb("wk_s", [P, HD])
        wv_s = sb("wv_s", [P, HD])
        wlb_s = sb("wlb_s", [P, LR_ROWS])
        wo_s = sb("wo_s", [P, PAIRS, D])
        win_init = sb("win_init", [P, PAIRS, CHUNK])
        wout_init = sb("wout_init", [P, PAIRS, CHUNK])
        woutT_init = sb("woutT_init", [P, PAIRS, CHUNK])
        wr_s = sb("wr_s", [P, E])
        br_s = sb("br_s", [1, E])
        ones_row = sb("ones_row", [1, P])
        w1_s = sb("w1_s", [P, E, F])
        b1_s = sb("b1_s", [P, E * FT])
        w2_s = sb("w2_s", [P, E, FT, D])
        b2_s = sb("b2_s", [E, D])
        id_s = sb("id_s", [P, P])
        sel_half_s = sb("sel_half_s", [LR_ROWS, P])
        sel_wd_s = sb("sel_wd_s", [LR_ROWS, 2 * PAIRS])
        sel_lr_s = sb("sel_lr_s", [LR_ROWS, 4 * PAIRS])
        tri_s = sb("tri_s", [P, E * E])
        x_s = sb("x_s", [P, TW, D])
        TILES = (STEPS + 1) * TW
        stats = sb("stats", [P, TILES, 6])
        mean = sb("mean", [P, TILES])
        spread = sb("spread", [P, TILES])
        var = sb("var", [P, TILES])
        rstd = sb("rstd", [P, TILES])
        xn = sb("xn", [P, TW, D])
        xnT = sb("xnT", [P, TOK])
        tanh_s = sb("tanh_s", [P, 2 * TOK])
        qkT = sb("qkT", [P, PAIRS, 2, BG, CHUNK])
        vT = sb("vT", [P, PAIRS, TOK])
        kv = sb("kv", [P, PAIRS, TW, 2, P])
        lr_sum = sb("lr_sum", [LR_ROWS, BG])
        lr_tanh = sb("lr_tanh", [LR_ROWS, TOK])
        lr_mean = sb("lr_mean", [LR_ROWS, BG])
        lr_wide = sb("lr_wide", [LR_ROWS, TW, P])
        wd_rhs = sb("wd_rhs", [LR_ROWS, 2 * PAIRS, BG])
        lr_tok = sb("lr_tok", [P, PAIRS, TW, 2, 2])
        wd_front = sb("wd_front", [P, 2 * PAIRS, BG])
        wd_rec = sb("wd_rec", [P, 2, PAIRS, BG])
        w_in = sb("w_in", [P, PAIRS, BG, P])
        w_out = sb("w_out", [P, PAIRS, BG, P])
        w_outT = sb("w_outT", [P, PAIRS, BG, P])
        nmax = sb("nmax", [P, 2, 4])
        ez = sb("ez", [P, 2, 4, CHUNK])
        esum = sb("esum", [P, 2, 4])
        erec = sb("erec", [P, 2, 4])
        pz = sb("pz", [P, 2, 4, CHUNK])
        p_tok = sb("p_tok", [P, 2, P])
        pa = sb("pa", [P, P])
        s_tok = sb("s_tok", [P, 2])
        g_tok = sb("g_tok", [P, 2, P])
        oT = sb("oT", [P, 2, P])
        x_all = [w.rearrange("p a b c -> p (a b c)").rearrange("p (c t d) -> p c t d", t=TW, d=D)
                 for w in (w_out[:], w_outT[:])]
        assert GROUPS == 2 and CHUNKS * TW == PAIRS * BG
        hbuf = sb("hbuf", [P, 2, FT, TOK])
        ngmax = sb("ngmax", [P, TW])
        gexp = sb("gexp", [P, TW, E])
        gsum = sb("gsum", [P, TW])
        grec = sb("grec", [P, TW])
        prob = sb("prob", [P, TW, E])
        gt = sb("gt", [P, TW, E, E])
        eq = sb("eq", [P, TW, E, E])
        cum = sb("cum", [P, TW, E])
        cnt = sb("cnt", [P, TW, E])
        keep = sb("keep", [P, TW, E])
        gate = sb("gate", [P, TW, E])
        gateT = sb("gateT", [E, TW * P])
        acc = sb("acc", [P, TW, D])
        acc_done = sb("acc_done", [P, TW, D])
        out_s = sb("out_s", [P, TW, D])

        b_proj = bank("b_proj")
        b_up = bank("b_up")
        b_misc = bank("b_misc")
        b_z = bank("b_z")
        b_a = bank("b_a")
        b_g = [bank("b_g0"), bank("b_g1")]
        b_y = bank("b_y")

        load = sem("load")
        x_all_load = [sem("x_all_load0"), sem("x_all_load1")]
        x_load = sem("x_load")
        consts_set = sem("consts_set")
        states_zero = sem("states_zero")
        stats_ready = sem("stats_ready")
        ln_chain = sem("ln_chain")
        var_ready = sem("var_ready")
        std_ready = sem("std_ready")
        w_halved = sem("w_halved")
        out_stored = sem("out_stored")
        xn_ready = sem("xn_ready")
        xnT_mm = sem("xnT_mm")
        xnT_ready = sem("xnT_ready")
        logits_mm = sem("logits_mm")
        lr_sum_ready = sem("lr_sum_ready")
        lr_mean_ready = sem("lr_mean_ready")
        lr_ready = sem("lr_ready")
        gmax_ready = sem("gmax_ready")
        gexp_ready = sem("gexp_ready")
        gate_chain = sem("gate_chain")
        sel_mm = sem("sel_mm")
        sel_ready = sem("sel_ready")
        wd_ready = sem("wd_ready")
        gateT_mm = sem("gateT_mm")
        gateT_ready = sem("gateT_ready")
        out_ready = sem("out_ready")
        qk_mm = sem("qk_mm")
        tanh_ready = sem("tanh_ready")
        qk_ready = sem("qk_ready")
        v_mm = sem("v_mm")
        vT_ready = sem("vT_ready")
        kv_mm = sem("kv_mm")
        kv_ready = sem("kv_ready")
        y_mm = sem("y_mm")
        y_used = sem("y_used")
        up_mm = sem("up_mm")
        h_ready = sem("h_ready")
        z_mm = sem("z_mm")
        max_ready = sem("max_ready")
        exp_ready = sem("exp_ready")
        erec_ready = sem("erec_ready")
        p_ready = sem("p_ready")
        a_mm = sem("a_mm")
        p_tok_ready = sem("p_tok_ready")
        s_ready = sem("s_ready")
        g_ready = sem("g_ready")
        attn_mm = sem("attn_mm")
        grad_mm = sem("grad_mm")
        state_ready = sem("state_ready")
        woutT_mm = sem("woutT_mm")
        woutT_ready = sem("woutT_ready")
        init_ready = sem("init_ready")
        GATE_LINKS = 11
        N_LOADS = 20

        def rows(a, group, c, half):
            b = group * BG + half
            return a[b:b + TW + 1:2, bass.ds(c * CHUNK, CHUNK), :].rearrange("w n d -> n w d")

        def is_first(T):
            return isinstance(T, int) and T == 0

        def slots(eng, slot):
            def step(T, s, front, lo, hi, start):
                def unit(lag):
                    r = s - LEAD - lag
                    return (T * SLOTS + r, r % SLOTS) if lo <= r < hi else None
                slot(T, s, front, start, unit)

            ALL = (-SLOTS - 8, SLOTS)
            for s in range(SLOTS):
                step(0, s, True, 0, SLOTS, True)
            with eng.Fori(1, CHUNKS) as T:
                for s in range(SLOTS):
                    step(T, s, True, *ALL, False)
            for g in range(1, GROUPS):
                for s in range(SLOTS):
                    step(g * CHUNKS, s, True, *ALL, True)
                with eng.Fori(g * CHUNKS + 1, (g + 1) * CHUNKS) as T:
                    for s in range(SLOTS):
                        step(T, s, True, *ALL, False)
            for s in range(LEAD + 3):
                step(STEPS, s, False, -SLOTS, 0, False)

        block = ctx.enter_context(nc.Block())

        @block.sync
        def _(eng):
            for batch in range(B):
                group, b = divmod(batch, BG)
                half = b % 2 * CHUNK
                eng.dma_start(x_all[group][half:half + CHUNK, :, b // 2],
                              x[batch].rearrange("(c n) d -> n c d", n=CHUNK)).then_inc(x_all_load[group], 16)
            for dst, src in ((wq_s[:], wqT), (wk_s[:], wkT), (wv_s[:], wvT), (wlb_s[:], wlbT), (id_s[:], ident),
                             (wr_s[:], wr), (br_s[:], br), (sel_half_s[:], sel_half), (sel_wd_s[:], sel_wd),
                             (sel_lr_s[:], sel_lr), (tri_s[:], tri), (b1_s[:], b1T), (b2_s[:], b2),
                             (win_init[:], winT0), (wout_init[:], wout0), (woutT_init[:], woutT0),
                             (w1_s[:], w1.rearrange("e d f -> d e f")),
                             (w2_s[:, 0:E // 2], w2[0:E // 2].rearrange("e (t f) d -> f e t d", f=P)),
                             (w2_s[:, E // 2:E], w2[E // 2:E].rearrange("e (t f) d -> f e t d", f=P)),
                             (wo_s[:], woT)):
                eng.dma_start(dst, src).then_inc(load, 16)

            def load_x(T, group, c):
                if not is_first(T):
                    eng.wait_ge(y_used, (T - 1) * E + 1)
                for half in range(2):
                    eng.dma_start(x_s[half * CHUNK:(half + 1) * CHUNK], rows(x, group, c, half)).then_inc(x_load, 16)

            def store(T, group, c):
                eng.wait_ge(out_ready, T + 1)
                for half in range(2):
                    eng.dma_start(rows(out, group, c, half), out_s[half * CHUNK:(half + 1) * CHUNK])\
                        .then_inc(out_stored, 16)

            load_x(0, 0, 0)
            load_x(1, 0, 1)
            for group in range(GROUPS):
                T0 = group * CHUNKS
                if group:
                    load_x(T0, group, 0)
                    store(T0 - 2, group - 1, CHUNKS - 2)
                    load_x(T0 + 1, group, 1)
                    store(T0 - 1, group - 1, CHUNKS - 1)
                with eng.Fori(1, CHUNKS - 1) as c:
                    load_x(c + (T0 + 1), group, c + 1)
                    store(c + (T0 - 1), group, c - 1)
            load_x(STEPS, GROUPS - 1, CHUNKS - 1)
            store(STEPS - 2, GROUPS - 1, CHUNKS - 2)
            store(STEPS - 1, GROUPS - 1, CHUNKS - 1)
            eng.wait_ge(out_stored, 32 * STEPS)

        @block.gpsimd
        def _(eng):
            eng.memset(stats[:, STEPS * TW:], 0.0)
            eng.memset(ones_row[:], 1.0).then_inc(consts_set, 1)
            eng.wait_ge(load, 16 * N_LOADS)
            eng.wait_ge(states_zero, 3)

            def start_states(T, g):
                pair, twin = divmod(g, TW)
                if T > 0:
                    eng.wait_ge(woutT_ready, (T - 1) * SLOTS + g + 1)
                for dst, src in ((w_in, win_init), (w_out, wout_init), (w_outT, woutT_init)):
                    for h in range(2):
                        c = slice(h * CHUNK, (h + 1) * CHUNK)
                        eng.tensor_copy(dst[c, pair, 2 * twin:2 * twin + 2, c],
                                        src[c, pair:pair + 1].broadcast_to([CHUNK, 2, CHUNK])).then_inc(init_ready, 1)

            def slot(T, s, front, start, unit):
                if start:
                    done = min(s + 5, SLOTS)
                    if T * SLOTS + s > LEAD:
                        eng.wait_ge(p_ready, T * SLOTS + s - LEAD)
                    for g in range(s + 4 if s else 0, done):
                        start_states(T, g)
                    eng.wait_ge(init_ready, (T // CHUNKS * SLOTS + done) * 6)
                if u := unit(0):
                    r, g = u
                    eng.wait_ge(erec_ready, r + 1)
                    if not (is_first(T) and g < 2):
                        eng.wait_ge(a_mm, r - 1)
                    eng.tensor_tensor(pz[:, g % 2], ez[:, g % 2],
                                      erec[:, g % 2].unsqueeze(2).broadcast_to([P, 4, CHUNK]),
                                      ALU.mult).then_inc(p_ready, 1)
            slots(eng, slot)

        @block.scalar
        def _(eng):
            eng.wait_ge(var_ready, 1)
            eng.activation(rstd[:], var[:], ACT.Sqrt).then_inc(std_ready, 1)

            eng.wait_ge(xnT_mm, 1)
            eng.activation(xnT[:], b_up[:, 0:TOK], ACT.Copy).then_inc(xnT_ready, 1)

            def slot(T, s, front, start, unit):
                first = is_first(T)
                j, odd = divmod(s, 2)
                if front and not odd:
                    eng.wait_ge(qk_mm, T * PAIRS + j + 1)
                    if not (first and s == 0):
                        eng.wait_ge(qk_ready, T * PAIRS + j)
                    eng.activation(tanh_s[:], b_proj[:], ACT.Tanh).then_inc(tanh_ready, 1)
                if front and odd:
                    eng.wait_ge(v_mm, T * PAIRS + j + 1)
                    eng.activation(vT[:, j], b_proj[:, 0:TOK], ACT.Copy).then_inc(vT_ready, 1)
                if u := unit(0):
                    r, g = u
                    eng.wait_ge(max_ready, r + 1)
                    if not (first and g < 2):
                        eng.wait_ge(p_ready, r - 1)
                    for n in range(4):
                        op = eng.activation(ez[:, g % 2, n], b_z[:, n * CHUNK:(n + 1) * CHUNK], ACT.Exp,
                                            bias=nmax[:, g % 2, n:n + 1], accum_out=esum[:, g % 2, n:n + 1])
                    op.then_inc(exp_ready, 1)
                if front:
                    e = j
                    eng.wait_ge(up_mm, T * SLOTS + s + 1)
                    if not (first and e < 2):
                        eng.wait_ge(y_mm, T * E + e - 1)
                    for n in range(2):
                        ft = 2 * odd + n
                        op = eng.activation(hbuf[:, e % 2, ft], b_up[:, n * TOK:(n + 1) * TOK], ACT.Relu,
                                            bias=b1_s[:, e * FT + ft:e * FT + ft + 1])
                    op.then_inc(h_ready, 1)
                if u := unit(3):
                    r, g = u
                    pair, twin = divmod(g, TW)
                    eng.wait_ge(woutT_mm, r + 1)
                    eng.activation(w_outT[:, pair, 2 * twin:2 * twin + 2], b_g[0][:, 2 * P:4 * P], ACT.Copy)\
                        .then_inc(woutT_ready, 1)
                if u := unit(1):
                    r, g = u
                    eng.wait_ge(a_mm, r + 1)
                    if not (first and g < 2):
                        eng.wait_ge(grad_mm, r - 1)
                    eng.activation(p_tok[:, g % 2], b_a[:, P:2 * P], ACT.Copy)
                    eng.activation(oT[:, g % 2], b_a[:, 2 * P:3 * P], ACT.Copy).then_inc(p_tok_ready, 1)
                if front and s == 0:
                    eng.wait_ge(gmax_ready, T + 1)
                    if not first:
                        eng.wait_ge(lr_mean_ready, T)
                    for b in range(BG):
                        op = eng.activation(lr_tanh[:, b * CHUNK:(b + 1) * CHUNK],
                                            b_misc[0:LR_ROWS, P + b * CHUNK:P + (b + 1) * CHUNK], ACT.Tanh,
                                            scale=0.5, accum_out=lr_sum[:, b:b + 1])
                    op.then_inc(lr_sum_ready, 1)
                    for t in range(TW):
                        op = eng.activation(gexp[:, t], b_misc[:, t * E:(t + 1) * E], ACT.Exp,
                                            bias=ngmax[:, t:t + 1], accum_out=gsum[:, t:t + 1])
                    op.then_inc(gexp_ready, 1)
                if front and s == 2:
                    eng.wait_ge(gateT_mm, T + 1)
                    eng.activation(gateT[:], b_misc[0:E, 0:TW * P], ACT.Copy).then_inc(gateT_ready, 1)
                if front and s == SLOTS - 1:
                    eng.wait_ge(xnT_mm, T + 2)
                    eng.activation(xnT[:], b_up[:, 0:TOK], ACT.Copy).then_inc(xnT_ready, 1)
            slots(eng, slot)

        @block.tensor
        def _(eng):
            def mm(o, a, b, start=True, stop=True, **kw):
                return eng.matmul(o, a, b, start=start, stop=stop, **kw)

            def transpose_xn():
                for t in range(TW):
                    op = eng.transpose(b_up[:, t * P:(t + 1) * P], xn[:, t], id_s[:])
                op.then_inc(xnT_mm, 1)

            eng.wait_ge(load, 16 * N_LOADS)
            eng.wait_ge(w_halved, 1)
            eng.wait_ge(consts_set, 1)
            eng.wait_ge(xn_ready, 1)
            transpose_xn()

            def slot(T, s, front, start, unit):
                first = is_first(T)
                j, odd = divmod(s, 2)
                e = j
                if front and not odd:
                    if s == 0:
                        eng.wait_ge(xnT_ready, T + 1)
                    if not (first and s == 0):
                        eng.wait_ge(kv_ready, T * PAIRS + j)
                    mm(b_proj[:, 0:TOK], wq_s[:, j * P:(j + 1) * P], xnT[:])
                    mm(b_proj[:, TOK:2 * TOK], wk_s[:, j * P:(j + 1) * P], xnT[:]).then_inc(qk_mm, 1)
                if front and odd:
                    eng.wait_ge(qk_ready, T * PAIRS + j + 1)
                    mm(b_proj[:, 0:TOK], wv_s[:, j * P:(j + 1) * P], xnT[:]).then_inc(v_mm, 1)
                if u := unit(0):
                    r, g = u
                    pair, twin = divmod(g, TW)
                    if start and s >= LEAD:
                        eng.wait_ge(init_ready, (T // CHUNKS * SLOTS + g + 1) * 6)
                    if not (first and g == 0):
                        eng.wait_ge(exp_ready, r)
                    for b in range(2):
                        op = mm(b_z[:, 0:4 * CHUNK].rearrange("p (a b n) -> p a b n", a=2, b=2)[:, :, b], w_in[:, pair, 2 * twin + b], qkT[:, pair, :, 2 * twin + b])
                    op.then_inc(z_mm, 1)
                if front and start and s == SLOTS - 1:
                    eng.wait_ge(init_ready, (T // CHUNKS + 1) * SLOTS * 6)
                if front:
                    if not (first and s == 0):
                        eng.wait_ge(h_ready, T * SLOTS + s)
                    for n in range(2):
                        f0 = (2 * odd + n) * P
                        op = mm(b_up[:, n * TOK:(n + 1) * TOK], w1_s[:, e, f0:f0 + P], xnT[:])
                    op.then_inc(up_mm, 1)
                if front and s == 0:
                    if not first:
                        eng.wait_ge(y_used, T * E)
                    for t in range(TW):
                        mm(b_misc[:, t * E:(t + 1) * E], xnT[:, t * P:(t + 1) * P], wr_s[:], stop=False)
                        mm(b_misc[:, t * E:(t + 1) * E], ones_row[:], br_s[:], start=False)
                    mm(b_misc[0:LR_ROWS, P:P + TOK], wlb_s[:], xnT[:]).then_inc(logits_mm, 1)
                if front and s == 1:
                    eng.wait_ge(lr_ready, T + 1)
                    eng.wait_ge(gexp_ready, T + 1)
                    mm(b_misc[:, 0:2 * PAIRS * BG], sel_half_s[:], wd_rhs[:].rearrange("r a b -> r (a b)"))
                    for t in range(TW):
                        o = 2 * PAIRS * BG + t * 4 * PAIRS
                        op = mm(b_misc[:, o:o + 4 * PAIRS], lr_wide[:, t], sel_lr_s[:])
                    op.then_inc(sel_mm, 1)
                if front and s == 2:
                    eng.wait_ge(gate_chain, (T + 1) * GATE_LINKS)
                    eng.wait_ge(y_used, T * E + 1)
                    for t in range(TW):
                        op = eng.transpose(b_misc[0:E, t * P:(t + 1) * P], gate[:, t], id_s[:])
                    op.then_inc(gateT_mm, 1)
                if u := unit(3):
                    r, g = u
                    pair, twin = divmod(g, TW)
                    eng.wait_ge(state_ready, r + 1)
                    for b in range(2):
                        op = eng.transpose(b_g[0][:, (2 + b) * P:(3 + b) * P], w_out[:, pair, 2 * twin + b], id_s[:])
                    op.then_inc(woutT_mm, 1)
                if u := unit(1):
                    r, g = u
                    pair, twin = divmod(g, TW)
                    if not (first and g == 0):
                        eng.wait_ge(g_ready, r)
                    for b in range(2):
                        n0 = twin * P + b * CHUNK
                        mm(b_a[b * CHUNK:(b + 1) * CHUNK, 0:P], vT[:, pair, n0:n0 + CHUNK],
                           w_outT[:, pair, 2 * twin + b])
                    eng.wait_ge(p_ready, r + 1)
                    for b in range(2):
                        mm(b_a[:, 2 * P + b * CHUNK:2 * P + (b + 1) * CHUNK], w_out[:, pair, 2 * twin + b],
                           pz[:, g % 2, b])
                    eng.transpose(b_a[:, P:2 * P], pz[:, g % 2, 2:4].rearrange("p a b -> p (a b)"), id_s[:]).then_inc(a_mm, 1)
                if front and odd:
                    eng.wait_ge(vT_ready, T * PAIRS + j + 1)
                    for t in range(TW):
                        eng.transpose(b_proj[:, 2 * t * P:(2 * t + 1) * P],
                                      qkT[:, j, 1, 2 * t:2 * t + 2].rearrange("p a b -> p (a b)"), id_s[:])
                        op = eng.transpose(b_proj[:, (2 * t + 1) * P:(2 * t + 2) * P],
                                           vT[:, j, t * P:(t + 1) * P], id_s[:])
                    op.then_inc(kv_mm, 1)
                if front and s == SLOTS - 1:
                    eng.wait_ge(h_ready, T * SLOTS + SLOTS)
                    eng.wait_ge(xn_ready, T + 2)
                    transpose_xn()
                if u := unit(2):
                    r, g = u
                    pair, twin = divmod(g, TW)
                    if g == 0:
                        if not first:
                            eng.wait_ge(out_ready, T)
                        mm(b_y[:, 0:P], gateT[:, 0:P], b2_s[:], stop=False, skip_group_check=True)
                        mm(b_y[:, P:2 * P], gateT[:, P:2 * P], b2_s[:], start=False, stop=False, skip_group_check=True)
                    eng.wait_ge(p_tok_ready, r + 1)
                    mm(b_y[:, twin * P:(twin + 1) * P], oT[:, g % 2], wo_s[:, pair], start=False,
                       stop=pair == PAIRS - 1, skip_group_check=True).then_inc(attn_mm, 1)
                    eng.wait_ge(g_ready, r + 1)
                    if not (first and g == 0):
                        eng.wait_ge(woutT_ready, r)
                    for b in range(2):
                        n = slice(b * CHUNK, (b + 1) * CHUNK)
                        mm(b_g[b][:, 0:P], kv[n, pair, twin, 0], g_tok[n, g % 2])
                    for b in range(2):
                        n = slice(b * CHUNK, (b + 1) * CHUNK)
                        op = mm(b_g[b][:, P:2 * P], p_tok[n, g % 2], kv[n, pair, twin, 1])
                    op.then_inc(grad_mm, 1)
                if front and odd:
                    eng.wait_ge(h_ready, T * SLOTS + s + 1)
                    if e == 0:
                        eng.wait_ge(sel_ready, T + 1)
                    else:
                        eng.wait_ge(y_used, T * E + e)
                    if e == 1:
                        eng.wait_ge(gateT_ready, T + 1)
                    for t in range(TW):
                        for ft in range(FT):
                            op = mm(b_misc[:, t * P:(t + 1) * P], hbuf[:, e % 2, ft, t * P:(t + 1) * P],
                                    w2_s[:, e, ft], start=ft == 0, stop=ft == FT - 1)
                    op.then_inc(y_mm, 1)
            slots(eng, slot)

        @block.vector
        def _(eng):
            def silu_weights():
                eng.wait_ge(load, 16 * N_LOADS)
                eng.tensor_scalar(wq_s[:], wq_s[:], 0.5, None, ALU.mult)
                eng.tensor_scalar(wk_s[:], wk_s[:], 0.5, None, ALU.mult).then_inc(w_halved, 1)

            def normalise(T):
                eng.wait_ge(x_load, 32 * (T + 1))
                for t in range(TW):
                    i = bass.ds(T * TW + t, 1)
                    op = eng.tensor_scalar(xn[:, t], x_s[:, t], mean[:, i], rstd[:, i], ALU.subtract, ALU.mult)
                op.then_inc(xn_ready, 1)

            eng.wait_ge(consts_set, 1)
            for group in range(GROUPS):
                eng.wait_ge(x_all_load[group], 16 * BG)
                with eng.Fori(0, CHUNKS * TW) as i:
                    eng.bn_stats(stats[:, bass.ds(i + group * CHUNKS * TW, 1)].rearrange("p a b -> p (a b)"),
                                 x_all[group].rearrange("p c t d -> p (c t) d")[:, bass.ds(i, 1)]
                                 .rearrange("p a b -> p (a b)")).then_inc(stats_ready, 1)
            eng.wait_ge(stats_ready, STEPS * TW)
            for state in (w_in, w_out, w_outT):
                eng.memset(state[:], 0.0).then_inc(states_zero, 1)
            links = [0]

            def link(op):
                links[0] += 1
                op.then_inc(ln_chain, 1)
                eng.wait_ge(ln_chain, links[0])
            link(eng.tensor_tensor(mean[:], stats[:, :, 1], stats[:, :, 4], ALU.add))
            link(eng.tensor_tensor(spread[:], stats[:, :, 1], stats[:, :, 4], ALU.subtract))
            link(eng.tensor_tensor(spread[:], spread[:], spread[:], ALU.mult))
            link(eng.tensor_scalar(spread[:], spread[:], 0.25, LN_EPS, ALU.mult, ALU.add))
            link(eng.tensor_tensor(var[:], stats[:, :, 2], stats[:, :, 5], ALU.add))
            link(eng.tensor_scalar(mean[:], mean[:], 0.5, None, ALU.mult))
            eng.scalar_tensor_tensor(var[:], var[:], 1.0 / D, spread[:], ALU.mult, ALU.add).then_inc(var_ready, 1)
            silu_weights()
            eng.wait_ge(std_ready, 1)
            link(eng.reciprocal(rstd[:], rstd[:]))
            normalise(0)

            def gates(T):
                n = [0]

                def link(op):
                    n[0] += 1
                    op.then_inc(gate_chain, 1)
                    eng.wait_ge(gate_chain, T * GATE_LINKS + n[0])

                all4 = [P, TW, E, E]
                of_j, of_i = prob[:].unsqueeze(2).broadcast_to(all4), prob[:].unsqueeze(3).broadcast_to(all4)
                link(eng.reciprocal(grec[:], gsum[:]))
                link(eng.tensor_tensor(prob[:], gexp[:], grec[:].unsqueeze(2).broadcast_to([P, TW, E]), ALU.mult))
                link(eng.tensor_tensor(gt[:], of_j, of_i, ALU.is_gt))
                link(eng.tensor_tensor(eq[:], of_j, of_i, ALU.is_equal))
                link(eng.tensor_tensor(eq[:].rearrange("p t i j -> p t (i j)"), eq[:].rearrange("p t i j -> p t (i j)"),
                                       tri_s[:].unsqueeze(1).broadcast_to([P, TW, E * E]), ALU.mult))
                link(eng.tensor_tensor(gt[:], gt[:], eq[:], ALU.add))
                eng.tensor_reduce(cnt[:], gt[:], AX.X, ALU.add)
                link(eng.tensor_tensor(eq[:], gt[:], of_j, ALU.mult))
                link(eng.tensor_reduce(cum[:], eq[:], AX.X, ALU.add))
                link(eng.tensor_scalar(keep[:], cum[:], TOP_P, None, ALU.is_lt))
                link(eng.scalar_tensor_tensor(keep[:], cnt[:], 1.5, keep[:], ALU.is_lt, ALU.max))
                link(eng.tensor_tensor(gate[:], keep[:], prob[:], ALU.mult))
                assert n[0] == GATE_LINKS

            def slot(T, s, front, start, unit):
                first = is_first(T)
                j, odd = divmod(s, 2)
                if u := unit(0):
                    r, g = u
                    eng.wait_ge(z_mm, r + 1)
                    if not (first and g < 2):
                        eng.wait_ge(exp_ready, r - 1)
                    eng.tensor_reduce(nmax[:, g % 2], b_z[:, 0:4 * CHUNK].rearrange("p (a b) -> p a b", b=CHUNK),
                                      AX.X, ALU.max, negate=True).then_inc(max_ready, 1)
                if front and not odd:
                    eng.wait_ge(tanh_ready, T * PAIRS + j + 1)
                    if not first:
                        eng.wait_ge(z_mm, (T - 1) * SLOTS + 2 * j + 2)
                    eng.scalar_tensor_tensor(qkT[:, j].rearrange("p a b c -> p (a b c)"), tanh_s[:], 1.0, b_proj[:],
                                             ALU.add, ALU.mult).then_inc(qk_ready, 1)
                if u := unit(0):
                    r, g = u
                    eng.wait_ge(exp_ready, r + 1)
                    if not (first and g < 2):
                        eng.wait_ge(p_ready, r - 1)
                    eng.reciprocal(erec[:, g % 2], esum[:, g % 2]).then_inc(erec_ready, 1)
                if front and s == 1:
                    eng.wait_ge(gexp_ready, T + 1)
                    gates(T)
                    eng.wait_ge(sel_mm, T + 1)
                    n = 2 * PAIRS * BG
                    eng.tensor_copy(wd_front[:].rearrange("p a b -> p (a b)"), b_misc[:, 0:n])
                    eng.tensor_copy(lr_tok[:].rearrange("p j t a b -> p t j (a b)"),
                                    b_misc[:, n:2 * n].rearrange("p (t j k) -> p t j k", t=TW, k=4))\
                        .then_inc(sel_ready, 1)
                if front and odd:
                    eng.wait_ge(kv_mm, T * PAIRS + j + 1)
                    if s == 1:
                        eng.wait_ge(sel_ready, T + 1)
                    if not first:
                        eng.wait_ge(grad_mm, (T - 1) * SLOTS + 2 * j + 2)
                    eng.tensor_tensor(kv[:, j].rearrange("p t a (h d) -> p (t a h) d", h=2),
                                      b_proj[:].rearrange("p (a d) -> p a d", d=CHUNK),
                                      lr_tok[:, j].rearrange("p t a b -> p (t a b)").unsqueeze(2)
                                      .broadcast_to([P, 8, CHUNK]), ALU.mult).then_inc(kv_ready, 1)
                if u := unit(1):
                    r, g = u
                    eng.wait_ge(p_tok_ready, r + 1)
                    if not (first and g < 2):
                        eng.wait_ge(grad_mm, r - 1)
                    for h in range(2):
                        c = slice(h * CHUNK, (h + 1) * CHUNK)
                        op = eng.tensor_tensor_reduce(out=pa[:, c], in0=b_a[:, c], in1=p_tok[:, g % 2, c], scale=1.0,
                                                      scalar=0.0, op0=ALU.mult, op1=ALU.add,
                                                      accum_out=s_tok[:, h:h + 1])
                    op.then_inc(s_ready, 1)
                    eng.wait_ge(s_ready, r + 1)
                    for h in range(2):
                        c = slice(h * CHUNK, (h + 1) * CHUNK)
                        op = eng.scalar_tensor_tensor(g_tok[:, g % 2, c], b_a[:, c], s_tok[:, h:h + 1],
                                                      p_tok[:, g % 2, c], ALU.subtract, ALU.mult)
                    op.then_inc(g_ready, 1)
                if front and s == SLOTS - 3:
                    eng.wait_ge(xnT_mm, T + 1)
                    normalise(T + 1)
                if u := unit(2):
                    r, g = u
                    pair, twin = divmod(g, TW)
                    if g == 0:
                        eng.tensor_copy(wd_rec[:].rearrange("p a b c -> p (a b) c"), wd_front[:])\
                            .then_inc(wd_ready, 1)
                        eng.wait_ge(wd_ready, T + 1)
                    eng.wait_ge(grad_mm, r + 1)
                    for n, state in enumerate((w_in, w_out)):
                        for b in range(2):
                            for h in range(2):
                                c = slice(h * CHUNK, (h + 1) * CHUNK)
                                block_ = state[c, pair, 2 * twin + b, c]
                                op = eng.scalar_tensor_tensor(
                                    block_, block_, wd_rec[c, n, pair, 2 * twin + b:2 * twin + b + 1],
                                    b_g[b][c, n * P + h * CHUNK:n * P + (h + 1) * CHUNK], ALU.mult, ALU.add)
                    op.then_inc(state_ready, 1)
                    if g == SLOTS - 1:
                        eng.wait_ge(attn_mm, r + 1)
                        eng.wait_ge(out_stored, 32 * (T - 1))
                        eng.tensor_tensor(out_s[:].rearrange("p t d -> p (t d)"), b_y[:, 0:TW * D],
                                          acc_done[:].rearrange("p t d -> p (t d)"), ALU.add).then_inc(out_ready, 1)
                if front and odd:
                    e = j
                    eng.wait_ge(y_mm, T * E + e + 1)
                    for t in range(TW):
                        before = acc[:, t]
                        if e == 0:
                            before = x_s[:, t]
                            eng.wait_ge(gate_chain, (T + 1) * GATE_LINKS)
                        op = eng.scalar_tensor_tensor((acc_done if e == E - 1 else acc)[:, t],
                                                      b_misc[:, t * P:(t + 1) * P], gate[:, t, e:e + 1],
                                                      before, ALU.mult, ALU.add)
                    op.then_inc(y_used, 1)
                if front and s == 0:
                    eng.wait_ge(logits_mm, T + 1)
                    eng.tensor_reduce(ngmax[:], b_misc[:, 0:TW * E].rearrange("p (a b) -> p a b", b=E), AX.X, ALU.max,
                                      negate=True).then_inc(gmax_ready, 1)
                    eng.wait_ge(lr_sum_ready, T + 1)
                    eng.tensor_scalar(lr_mean[:], lr_sum[:], 0.5 / CHUNK, 0.5, ALU.mult, ALU.add)\
                        .then_inc(lr_mean_ready, 1)
                    eng.wait_ge(lr_mean_ready, T + 1)
                    eng.tensor_tensor(wd_rhs[:], lr_mean[:].unsqueeze(1).broadcast_to([LR_ROWS, 2 * PAIRS, BG]),
                                      sel_wd_s[:].unsqueeze(2).broadcast_to([LR_ROWS, 2 * PAIRS, BG]), ALU.mult)
                    eng.tensor_copy(lr_wide[:].rearrange("r t (b n) -> r (t b) n", b=2),
                                    lr_mean[:].unsqueeze(2).broadcast_to([LR_ROWS, BG, CHUNK])).then_inc(lr_ready, 1)
            slots(eng, slot)


def kernel(**inputs):
    import numpy as np
    import concourse.bacc as _bacc
    from concourse import mybir as _mybir
    from concourse.bass_utils import run_bass_kernel_spmd as _run

    a = {k.split("_", 1)[1]: np.asarray(v) for k, v in inputs.items()}
    B, L, D = a["attn_x"].shape
    _, DI, H, DH = a["attn_W_in_init"].shape
    E, _, F = a["ffn_W1"].shape
    pairs = H // 2

    def by_pairs(w):
        return w.reshape(pairs, 2 * w.shape[1], w.shape[2]).transpose(1, 0, 2)

    w_in0 = a["attn_W_in_init"][0].transpose(1, 2, 0)
    w_out0 = a["attn_W_out_init"][0].transpose(1, 0, 2)
    rows = np.arange(4 * H)
    kind, head = rows // H, rows % H
    sel_half = (head[:, None] % 2 == np.arange(128)[None] // 64).astype(np.float32)
    cols = np.arange(2 * pairs)
    sel_wd = ((kind[:, None] == 2 + cols[None] // pairs) & (head[:, None] // 2 == cols[None] % pairs)) * np.float32(0.9)
    cols = np.arange(4 * pairs)
    sel_lr = ((head[:, None] == cols[None] // 4 * 2 + cols[None] % 2)
              & (kind[:, None] == cols[None] // 2 % 2)) * np.float32(0.001)
    tri = np.broadcast_to(np.tril(np.ones((E, E), np.float32)).reshape(1, -1), (128, E * E))
    arrays = {
        "x": a["attn_x"], "wqT": a["attn_Wq"].T, "wkT": a["attn_Wk"].T, "wvT": a["attn_Wv"].T,
        "wlbT": np.concatenate([a["attn_Wlr"], a["attn_Wbeta"]]).T,
        "woT": a["attn_Wo"].T.reshape(pairs, 128, D).transpose(1, 0, 2),
        "winT0": by_pairs(w_in0), "wout0": by_pairs(w_out0), "woutT0": by_pairs(w_out0.transpose(0, 2, 1)),
        "wr": a["ffn_Wr"], "br": a["ffn_br"][None], "w1": a["ffn_W1"],
        "b1T": a["ffn_b1"].reshape(E * F // 128, 128).T, "w2": a["ffn_W2"], "b2": a["ffn_b2"],
        "ident": np.eye(128, dtype=np.float32), "sel_half": sel_half, "sel_wd": sel_wd.astype(np.float32),
        "sel_lr": sel_lr.astype(np.float32), "tri": tri,
    }
    nc = _bacc.Bacc("TRN2", target_bir_lowering=False, num_devices=1)
    given = {f"in_{k}": np.ascontiguousarray(v) for k, v in arrays.items()}
    aps = {k: nc.dram_tensor(f"in_{k}", given[f"in_{k}"].shape, _mybir.dt.from_np(given[f"in_{k}"].dtype),
                             kind="ExternalInput").ap() for k in arrays}
    aps["out"] = nc.dram_tensor("out", (B, L, D), _mybir.dt.float32, kind="ExternalOutput").ap()
    build(nc, **aps)
    r = _run(nc, [given], core_ids=[0])
    return r.results[0]["out"]
```

```python
import concourse.bass as bass
from concourse import mybir
from concourse.alu_op_type import AluOpType as ALU
from contextlib import ExitStack

F32 = mybir.dt.float32
F32R = mybir.dt.float32r
ACT = mybir.ActivationFunctionType
AX = mybir.AxisListType

P = 128
CHUNK = 64
SLOTS = 16
LEAD = 8
LAST_LAG = 4
BASE_LR, BASE_WD = 0.001, 0.9
TOP_P = 0.8
LN_EPS = 1e-5


def build(nc, x, wqT, wkT, wvT, wlbT, woT, winT0, wout0, woutT0, wr, br, w1, b1T, w2, b2,
          ident, sel_half, sel_wd, sel_lr, tri, out):
    B, L, D = x.shape
    HD = wqT.shape[1]
    PAIRS = HD // P
    E, _, F = w1.shape
    FT = F // P
    CHUNKS = L // CHUNK
    BG = 4
    GROUPS = B // BG
    TW = 2
    TOK = BG * CHUNK
    STEPS = GROUPS * CHUNKS
    LR_ROWS = wlbT.shape[1]
    RING = PAIRS
    assert D == P and HD == 2 * F and F == TW * 2 * P and PAIRS * TW == SLOTS and E * 2 == SLOTS and FT == 4

    ctx = ExitStack()
    with ctx:
        def sb(name, shape, dt=F32):
            return ctx.enter_context(nc.sbuf_tensor(name, shape, dt))

        def bank(name):
            return ctx.enter_context(nc.psum_tensor(name, [P, 512], F32))

        def sem(name):
            return ctx.enter_context(nc.semaphore(name))

        wq_s = [sb("wq_hi", [P, HD], F32R), sb("wq_lo", [P, HD], F32R)]
        wk_s = [sb("wk_hi", [P, HD], F32R), sb("wk_lo", [P, HD], F32R)]
        wv_s = [sb("wv_hi", [P, HD], F32R), sb("wv_lo", [P, HD], F32R)]
        wlb_s = sb("wlb_s", [P, LR_ROWS])
        wo_s = sb("wo_s", [P, PAIRS, D])
        win_init = sb("win_init", [P, PAIRS, CHUNK])
        wout_init = sb("wout_init", [P, PAIRS, CHUNK])
        woutT_init = sb("woutT_init", [P, PAIRS, CHUNK])
        wr_s = sb("wr_s", [P, E])
        br_s = sb("br_s", [1, E])
        ones_row = sb("ones_row", [1, P])
        w1_s = [sb("w1_hi", [P, E, F], F32R), sb("w1_lo", [P, E, F], F32R)]
        b1_s = sb("b1_s", [P, E * FT])
        w2_s = sb("w2_s", [P, E, FT, D])
        b2_s = sb("b2_s", [E, D])
        id_s = sb("id_s", [P, P])
        sel_half_s = sb("sel_half_s", [LR_ROWS, P])
        sel_wd_s = sb("sel_wd_s", [LR_ROWS, 2 * PAIRS])
        sel_lr_s = sb("sel_lr_s", [LR_ROWS, 4 * PAIRS])
        tri_s = sb("tri_s", [P, E * E])
        x_s = sb("x_s", [P, TW, D])
        stats = sb("stats", [P, TW, 6])
        mean = sb("mean", [P, TW])
        spread = sb("spread", [P, TW])
        var_eps = sb("var_eps", [P, TW])
        minus_half = sb("minus_half", [P, TW])
        rstd = sb("rstd", [P, TW])
        newton = sb("newton", [P, TW])
        xn = sb("xn", [P, TW, D])
        xnT = sb("xnT", [P, TOK])
        xnT_s = [sb("xnT_hi", [P, TOK], F32R), sb("xnT_lo", [P, TOK], F32R)]
        tanh_s = sb("tanh_s", [P, 2 * TOK])
        qkT = sb("qkT", [P, PAIRS, 2, BG, CHUNK])
        vT = sb("vT", [P, PAIRS, TOK])
        kv = sb("kv", [P, PAIRS, TW, 2, P])
        raw = kv[:].rearrange("p j t a d -> p j (t a d)")
        lr_sum = sb("lr_sum", [LR_ROWS, BG])
        lr_mean = sb("lr_mean", [LR_ROWS, BG])
        lr_wide = sb("lr_wide", [LR_ROWS, TW, P])
        wd_rhs = sb("wd_rhs", [LR_ROWS, 2 * PAIRS, BG])
        lr_tok = sb("lr_tok", [P, PAIRS, TW, 2, 2])
        wd_front = sb("wd_front", [P, 2 * PAIRS, BG])
        wd_rec = sb("wd_rec", [P, 2, PAIRS, BG])
        w_io = sb("w_io", [P, 2, PAIRS, BG, P])
        w_in = w_io[:, 0]
        w_out = w_io[:, 1]
        w_outT = sb("w_outT", [P, PAIRS, BG, P])
        nmax = sb("nmax", [P, 2, 4])
        ez = sb("ez", [P, 2, 4, CHUNK])
        esum = sb("esum", [P, 2, 4])
        erec = sb("erec", [P, 2, 4])
        pz = sb("pz", [P, 2, 4, CHUNK])
        p_tok = sb("p_tok", [P, 2, P])
        pa = sb("pa", [P, P])
        s_tok = sb("s_tok", [P, 2])
        g_tok = sb("g_tok", [P, 2, P])
        oT = sb("oT", [P, 2, P])
        hbuf = sb("hbuf", [P, 2, FT, TOK])
        ngmax = sb("ngmax", [P, TW])
        gexp = sb("gexp", [P, TW, E])
        gsum = sb("gsum", [P, TW])
        grec = sb("grec", [P, TW])
        prob = sb("prob", [P, TW, E])
        gt = sb("gt", [P, TW, E, E])
        eq = sb("eq", [P, TW, E, E])
        cum = sb("cum", [P, TW, E])
        cnt = sb("cnt", [P, TW, E])
        keep = sb("keep", [P, TW, E])
        gate = sb("gate", [P, TW, E])
        gateT = sb("gateT", [E, TW * P])
        acc = sb("acc", [P, TW, D])
        acc_done = sb("acc_done", [P, TW, D])
        out_s = sb("out_s", [P, TW, D])

        b_proj = bank("b_proj")
        b_up = bank("b_up")
        b_misc = bank("b_misc")
        b_z = bank("b_z")
        b_a = bank("b_a")
        b_g = ctx.enter_context(nc.psum_tensor("b_g", [P, 2, 512], F32))
        b_y = bank("b_y")

        load = sem("load")
        load_front = sem("load_front")
        raw_load = [sem(f"raw_load{i}") for i in range(RING)]
        hi_ready = sem("hi_ready")
        lo_ready = sem("lo_ready")
        x_load = sem("x_load")
        consts_set = sem("consts_set")
        states_zero = sem("states_zero")
        ln_chain = sem("ln_chain")
        var_ready = sem("var_ready")
        rstd_guess = sem("rstd_guess")
        out_stored = sem("out_stored")
        xn_ready = sem("xn_ready")
        xnT_mm = sem("xnT_mm")
        xnT_copied = sem("xnT_copied")
        xnT_ready = sem("xnT_ready")
        logits_mm = sem("logits_mm")
        lr_sum_ready = sem("lr_sum_ready")
        lr_mean_ready = sem("lr_mean_ready")
        lr_ready = sem("lr_ready")
        gmax_ready = sem("gmax_ready")
        gexp_ready = sem("gexp_ready")
        gate_chain = sem("gate_chain")
        sel_mm = sem("sel_mm")
        sel_ready = sem("sel_ready")
        wd_ready = sem("wd_ready")
        gateT_mm = sem("gateT_mm")
        gateT_ready = sem("gateT_ready")
        out_ready = sem("out_ready")
        qk_mm = sem("qk_mm")
        tanh_ready = sem("tanh_ready")
        qk_ready = sem("qk_ready")
        v_mm = sem("v_mm")
        vT_ready = sem("vT_ready")
        kv_mm = sem("kv_mm")
        kv_ready = sem("kv_ready")
        y_mm = sem("y_mm")
        y_used = sem("y_used")
        up_mm = sem("up_mm")
        h_ready = sem("h_ready")
        z_mm = sem("z_mm")
        max_ready = sem("max_ready")
        exp_ready = sem("exp_ready")
        erec_ready = sem("erec_ready")
        p_ready = sem("p_ready")
        a_mm = sem("a_mm")
        p_tok_ready = sem("p_tok_ready")
        s_ready = sem("s_ready")
        decayed = sem("decayed")
        g_ready = sem("g_ready")
        attn_mm = sem("attn_mm")
        grad_mm = sem("grad_mm")
        state_ready = sem("state_ready")
        woutT_mm = sem("woutT_mm")
        woutT_ready = sem("woutT_ready")
        init_ready = sem("init_ready")
        GATE_LINKS = 11
        LN_LINKS = 8
        halves = (slice(0, F), slice(F, 2 * F))
        SPLIT = [(w[:, c], [t[:, c] for t in parts], scale) for w, parts, scale in
                 ((wqT, wq_s, 0.5), (wkT, wk_s, 0.5), (wvT, wv_s, 1.0)) for c in halves]
        SPLIT += [(w1[e], [t[:, e] for t in w1_s], 1.0) for e in range(E)]
        N_LOADS, N_LOADS_FRONT = 7, 8

        def rows(a, group, c, half):
            b = group * BG + half
            return a[b:b + TW + 1:2, bass.ds(c * CHUNK, CHUNK), :].rearrange("w n d -> n w d")

        def is_first(T):
            return isinstance(T, int) and T == 0

        def expert_tile(T, s, front, lag):
            i = s - 2 - lag
            if (front and i >= 0) or (i < 0 and not is_first(T)):
                return (T * SLOTS + i, *divmod(i % SLOTS, TW))

        def slots(eng, slot):
            def step(T, s, front, lo, hi, start):
                def unit(lag):
                    r = s - LEAD - lag
                    return (T * SLOTS + r, r % SLOTS) if lo <= r < hi else None
                slot(T, s, front, start, unit)

            ALL = (-SLOTS - 8, SLOTS)
            for s in range(SLOTS):
                step(0, s, True, 0, SLOTS, True)
            with eng.Fori(1, CHUNKS) as T:
                for s in range(SLOTS):
                    step(T, s, True, *ALL, False)
            for g in range(1, GROUPS):
                for s in range(SLOTS):
                    step(g * CHUNKS, s, True, *ALL, True)
                with eng.Fori(g * CHUNKS + 1, (g + 1) * CHUNKS) as T:
                    for s in range(SLOTS):
                        step(T, s, True, *ALL, False)
            for s in range(LEAD + LAST_LAG):
                step(STEPS, s, False, -SLOTS, 0, False)

        block = ctx.enter_context(nc.Block())

        @block.sync
        def _(eng):
            def load_x(T, group, c):
                if not is_first(T):
                    eng.wait_ge(y_used, (T - 1) * SLOTS + 2)
                for half in range(2):
                    eng.dma_start(x_s[half * CHUNK:(half + 1) * CHUNK], rows(x, group, c, half)).then_inc(x_load, 16)

            def store(T, group, c):
                eng.wait_ge(out_ready, T + 1)
                for half in range(2):
                    eng.dma_start(rows(out, group, c, half), out_s[half * CHUNK:(half + 1) * CHUNK])\
                        .then_inc(out_stored, 16)

            def load_chunk(n):
                if n >= RING:
                    eng.wait_ge(lo_ready, n - RING + 1)
                eng.dma_start(raw[:, n % RING], SPLIT[n][0]).then_inc(raw_load[n % RING], 16)

            load_x(0, 0, 0)
            for n in range(RING):
                load_chunk(n)
            for n in range(RING, len(SPLIT)):
                load_chunk(n)

            load_x(1, 0, 1)
            for group in range(GROUPS):
                T0 = group * CHUNKS
                if group:
                    load_x(T0, group, 0)
                    store(T0 - 2, group - 1, CHUNKS - 2)
                    load_x(T0 + 1, group, 1)
                    store(T0 - 1, group - 1, CHUNKS - 1)
                with eng.Fori(1, CHUNKS - 1) as c:
                    load_x(c + (T0 + 1), group, c + 1)
                    store(c + (T0 - 1), group, c - 1)
            load_x(STEPS, GROUPS - 1, CHUNKS - 1)
            store(STEPS - 2, GROUPS - 1, CHUNKS - 2)
            store(STEPS - 1, GROUPS - 1, CHUNKS - 1)
            eng.wait_ge(out_stored, 32 * STEPS)

        @block.gpsimd
        def _(eng):
            eng.memset(minus_half[:], -0.5)
            eng.memset(ones_row[:], 1.0).then_inc(consts_set, 1)
            eng.wait_ge(consts_set, 1)

            def guess_rstd(T):
                eng.wait_ge(var_ready, T + 1)
                eng.tensor_tensor(rstd[:], var_eps[:], minus_half[:], ALU.pow).then_inc(rstd_guess, 1)

            guess_rstd(0)
            eng.wait_ge(rstd_guess, 1)
            eng.wait_ge(load, 16 * N_LOADS)
            eng.wait_ge(states_zero, 2)

            def start_states(T, g):
                pair, twin = divmod(g, TW)
                if T > 0:
                    eng.wait_ge(woutT_ready, (T - 1) * SLOTS + g + 1)
                for dst, src in ((w_in, win_init), (w_out, wout_init), (w_outT, woutT_init)):
                    for h in range(2):
                        c = slice(h * CHUNK, (h + 1) * CHUNK)
                        eng.tensor_copy(dst[c, pair, 2 * twin:2 * twin + 2, c],
                                        src[c, pair:pair + 1].broadcast_to([CHUNK, 2, CHUNK])).then_inc(init_ready, 1)

            def slot(T, s, front, start, unit):
                if start:
                    done = min(s + 4, SLOTS)
                    if T * SLOTS + s > LEAD:
                        eng.wait_ge(decayed, T * SLOTS + s - LEAD - 1)
                        eng.wait_ge(p_ready, T * SLOTS + s - LEAD)
                    for g in range(s + 3 if s else 0, done):
                        start_states(T, g)
                    eng.wait_ge(init_ready, (T // CHUNKS * SLOTS + done) * 6)
                if u := unit(0):
                    r, g = u
                    eng.wait_ge(erec_ready, r + 1)
                    if not (is_first(T) and g < 2):
                        eng.wait_ge(a_mm, r - 1)
                    eng.tensor_tensor(pz[:, g % 2], ez[:, g % 2],
                                      erec[:, g % 2].unsqueeze(2).broadcast_to([P, 4, CHUNK]),
                                      ALU.mult).then_inc(p_ready, 1)
                if u := unit(1):
                    r, g = u
                    pair, twin = divmod(g, TW)
                    bs = slice(2 * twin, 2 * twin + 2)
                    if g == 0:
                        eng.wait_ge(wd_ready, T + 1)
                    eng.wait_ge(a_mm, r + 1)
                    eng.tensor_tensor(w_io[:, :, pair, bs], w_io[:, :, pair, bs],
                                      wd_rec[:, :, pair, bs].unsqueeze(3).broadcast_to([P, 2, 2, P]),
                                      ALU.mult).then_inc(decayed, 1)
                if front and s == SLOTS - 4:
                    guess_rstd(T + 1)
            slots(eng, slot)

        @block.scalar
        def _(eng):
            for dst, src in ((id_s[:], ident), (b1_s[:], b1T), (wlb_s[:], wlbT), (wr_s[:], wr), (br_s[:], br),
                             (sel_half_s[:], sel_half), (sel_wd_s[:], sel_wd), (sel_lr_s[:], sel_lr)):
                eng.dma_start(dst, src).then_inc(load_front, 16)
            for dst, src in ((tri_s[:], tri), (b2_s[:], b2), (w2_s[:], w2.rearrange("e (t f) d -> f e t d", f=P)),
                             (win_init[:], winT0), (wout_init[:], wout0), (woutT_init[:], woutT0), (wo_s[:], woT)):
                eng.dma_start(dst, src).then_inc(load, 16)

            for n, (_, parts, scale) in enumerate(SPLIT):
                eng.wait_ge(raw_load[n % RING], 16 * (n // RING + 1))
                eng.activation(parts[0], raw[:, n % RING], ACT.Copy, scale=scale).then_inc(hi_ready, 1)

            def copy_xnT(T):
                eng.wait_ge(xnT_mm, T + 1)
                eng.activation(xnT[:], b_up[:, 0:TOK], ACT.Copy)
                eng.activation(xnT_s[0][:], b_up[:, 0:TOK], ACT.Copy).then_inc(xnT_copied, 1)

            copy_xnT(0)

            def slot(T, s, front, start, unit):
                first = is_first(T)
                j, odd = divmod(s, 2)
                if u := unit(0):
                    r, g = u
                    eng.wait_ge(max_ready, r + 1)
                    if not (first and g < 2):
                        eng.wait_ge(p_ready, r - 1)
                    for n in range(4):
                        op = eng.activation(ez[:, g % 2, n], b_z[:, n * CHUNK:(n + 1) * CHUNK], ACT.Exp,
                                            bias=nmax[:, g % 2, n:n + 1], accum_out=esum[:, g % 2, n:n + 1])
                    op.then_inc(exp_ready, 1)
                if u := unit(LAST_LAG):
                    r, g = u
                    pair, twin = divmod(g, TW)
                    eng.wait_ge(woutT_mm, r + 1)
                    eng.activation(w_outT[:, pair, 2 * twin:2 * twin + 2], b_z[:, 2 * P:4 * P], ACT.Copy)\
                        .then_inc(woutT_ready, 1)
                if front and not odd:
                    eng.wait_ge(qk_mm, T * PAIRS + j + 1)
                    if not (first and s == 0):
                        eng.wait_ge(qk_ready, T * PAIRS + j)
                    eng.activation(tanh_s[:], b_proj[:], ACT.Tanh).then_inc(tanh_ready, 1)
                if front and odd:
                    eng.wait_ge(v_mm, T * PAIRS + j + 1)
                    eng.activation(vT[:, j], b_proj[:, 0:TOK], ACT.Copy).then_inc(vT_ready, 1)
                if u := unit(1):
                    r, g = u
                    eng.wait_ge(a_mm, r + 1)
                    if not (first and g < 2):
                        eng.wait_ge(grad_mm, r - 1)
                        eng.wait_ge(attn_mm, r - 1)
                    eng.activation(p_tok[:, g % 2], b_a[:, P:2 * P], ACT.Copy)
                    eng.activation(oT[:, g % 2], b_a[:, 2 * P:3 * P], ACT.Copy).then_inc(p_tok_ready, 1)
                if front and s == 0:
                    eng.wait_ge(gmax_ready, T + 1)
                    if not first:
                        eng.wait_ge(lr_mean_ready, T)
                    for b in range(BG):
                        logits = b_misc[0:LR_ROWS, P + b * CHUNK:P + (b + 1) * CHUNK]
                        op = eng.activation(logits, logits, ACT.Tanh,
                                            scale=0.5, accum_out=lr_sum[:, b:b + 1])
                    op.then_inc(lr_sum_ready, 1)
                    for t in range(TW):
                        op = eng.activation(gexp[:, t], b_misc[:, t * E:(t + 1) * E], ACT.Exp,
                                            bias=ngmax[:, t:t + 1], accum_out=gsum[:, t:t + 1])
                    op.then_inc(gexp_ready, 1)
                if front and s == 3:
                    eng.wait_ge(gateT_mm, T + 1)
                    eng.activation(gateT[:], b_misc[0:E, 0:TW * P], ACT.Copy).then_inc(gateT_ready, 1)
                if front:
                    e = j
                    eng.wait_ge(up_mm, T * SLOTS + s + 1)
                    if not (first and e < 2):
                        eng.wait_ge(y_mm, T * SLOTS + 2 * e - 2)
                    for n in range(2):
                        ft = 2 * odd + n
                        op = eng.activation(hbuf[:, e % 2, ft], b_up[:, n * TOK:(n + 1) * TOK], ACT.Relu,
                                            bias=b1_s[:, e * FT + ft:e * FT + ft + 1])
                    op.then_inc(h_ready, 1)
                if front and s == SLOTS - 1:
                    copy_xnT(T + 1)
            slots(eng, slot)

        @block.tensor
        def _(eng):
            def mm(o, a, b, start=True, stop=True, **kw):
                return eng.matmul(o, a, b, start=start, stop=stop, **kw)

            def transpose_xn():
                for t in range(TW):
                    op = eng.transpose(b_up[:, t * P:(t + 1) * P], xn[:, t], id_s[:])
                op.then_inc(xnT_mm, 1)

            def mm3(o, a, b):
                mm(o, a[0], b[0][:], stop=False)
                mm(o, a[0], b[1][:], start=False, stop=False)
                return mm(o, a[1], b[0][:], start=False)

            eng.wait_ge(load_front, 16 * N_LOADS_FRONT)
            eng.wait_ge(consts_set, 1)
            eng.wait_ge(xn_ready, 1)
            transpose_xn()

            def slot(T, s, front, start, unit):
                first = is_first(T)
                j, odd = divmod(s, 2)
                e = j
                if first:
                    if s == 0:
                        eng.wait_ge(lo_ready, 6)
                if u := unit(LAST_LAG):
                    r, g = u
                    pair, twin = divmod(g, TW)
                    eng.wait_ge(state_ready, r + 1)
                    eng.wait_ge(exp_ready, r + LAST_LAG if unit(0) else T * SLOTS)
                    if not (first and g == 0):
                        eng.wait_ge(woutT_ready, r)
                    for b in range(2):
                        op = eng.transpose(b_z[:, (2 + b) * P:(3 + b) * P], w_out[:, pair, 2 * twin + b], id_s[:])
                    op.then_inc(woutT_mm, 1)
                if u := unit(0):
                    r, g = u
                    pair, twin = divmod(g, TW)
                    if start and s >= LEAD:
                        eng.wait_ge(init_ready, (T // CHUNKS * SLOTS + g + 1) * 6)
                    if not (first and g == 0):
                        eng.wait_ge(exp_ready, r)
                    for b in range(2):
                        op = mm(b_z[:, 0:4 * CHUNK].rearrange("p (a b n) -> p a b n", a=2, b=2)[:, :, b],
                                w_in[:, pair, 2 * twin + b], qkT[:, pair, :, 2 * twin + b])
                    op.then_inc(z_mm, 1)
                if front and start and s == SLOTS - 1:
                    eng.wait_ge(init_ready, (T // CHUNKS + 1) * SLOTS * 6)
                if u := unit(2):
                    r, g = u
                    pair, twin = divmod(g, TW)
                    eng.wait_ge(g_ready, r + 1)
                    if not (first and g == 0):
                        eng.wait_ge(state_ready, r)
                    for b in range(2):
                        n = slice(b * CHUNK, (b + 1) * CHUNK)
                        mm(b_g[:, b, 0:P], kv[n, pair, twin, 0], g_tok[n, g % 2])
                    for b in range(2):
                        n = slice(b * CHUNK, (b + 1) * CHUNK)
                        op = mm(b_g[:, b, P:2 * P], p_tok[n, g % 2], kv[n, pair, twin, 1])
                    op.then_inc(grad_mm, 1)
                    if g == 0:
                        if not first:
                            eng.wait_ge(out_ready, T)
                        mm(b_y[:, 0:P], gateT[:, 0:P], b2_s[:], stop=False, skip_group_check=True)
                        mm(b_y[:, P:2 * P], gateT[:, P:2 * P], b2_s[:], start=False, stop=False, skip_group_check=True)
                    eng.wait_ge(p_tok_ready, r + 1)
                    mm(b_y[:, twin * P:(twin + 1) * P], oT[:, g % 2], wo_s[:, pair], start=False,
                       stop=pair == PAIRS - 1, skip_group_check=True).then_inc(attn_mm, 1)
                if front and not odd:
                    if s == 0:
                        eng.wait_ge(xnT_ready, T + 1)
                    if not (first and s == 0):
                        eng.wait_ge(kv_ready, T * PAIRS + j)
                    c = slice(j * P, (j + 1) * P)
                    mm3(b_proj[:, 0:TOK], [w[:, c] for w in wq_s], xnT_s)
                    mm3(b_proj[:, TOK:2 * TOK], [w[:, c] for w in wk_s], xnT_s).then_inc(qk_mm, 1)
                if front and odd:
                    eng.wait_ge(qk_ready, T * PAIRS + j + 1)
                    c = slice(j * P, (j + 1) * P)
                    mm3(b_proj[:, 0:TOK], [w[:, c] for w in wv_s], xnT_s).then_inc(v_mm, 1)
                if u := unit(1):
                    r, g = u
                    pair, twin = divmod(g, TW)
                    if not (first and g == 0):
                        eng.wait_ge(g_ready, r)
                    for b in range(2):
                        n0 = twin * P + b * CHUNK
                        mm(b_a[b * CHUNK:(b + 1) * CHUNK, 0:P], vT[:, pair, n0:n0 + CHUNK],
                           w_outT[:, pair, 2 * twin + b])
                    eng.wait_ge(p_ready, r + 1)
                    for b in range(2):
                        mm(b_a[:, 2 * P + b * CHUNK:2 * P + (b + 1) * CHUNK], w_out[:, pair, 2 * twin + b],
                           pz[:, g % 2, b])
                    eng.transpose(b_a[:, P:2 * P], pz[:, g % 2, 2:4].rearrange("p a b -> p (a b)"), id_s[:])\
                        .then_inc(a_mm, 1)
                if front and s == 0:
                    if not first:
                        eng.wait_ge(y_used, T * SLOTS - 2)
                    for t in range(TW):
                        mm(b_misc[:, t * E:(t + 1) * E], xnT[:, t * P:(t + 1) * P], wr_s[:], stop=False)
                        mm(b_misc[:, t * E:(t + 1) * E], ones_row[:], br_s[:], start=False)
                    mm(b_misc[0:LR_ROWS, P:P + TOK], wlb_s[:], xnT[:]).then_inc(logits_mm, 1)
                if front and s == 1:
                    eng.wait_ge(lr_ready, T + 1)
                    if first:
                        eng.wait_ge(gexp_ready, 1)
                    else:
                        eng.wait_ge(y_used, T * SLOTS - 1)
                    mm(b_misc[:, 0:2 * PAIRS * BG], sel_half_s[:], wd_rhs[:].rearrange("r a b -> r (a b)"))
                    for t in range(TW):
                        o = 2 * PAIRS * BG + t * 4 * PAIRS
                        op = mm(b_misc[:, o:o + 4 * PAIRS], lr_wide[:, t], sel_lr_s[:])
                    op.then_inc(sel_mm, 1)
                if front and s == 3:
                    eng.wait_ge(gate_chain, (T + 1) * GATE_LINKS)
                    eng.wait_ge(y_used, T * SLOTS + 1)
                    for t in range(TW):
                        op = eng.transpose(b_misc[0:E, t * P:(t + 1) * P], gate[:, t], id_s[:])
                    op.then_inc(gateT_mm, 1)
                if front:
                    if first and not odd:
                        eng.wait_ge(lo_ready, 6 + e + 1)
                    if not (first and s == 0):
                        eng.wait_ge(h_ready, T * SLOTS + s)
                    for n in range(2):
                        f0 = (2 * odd + n) * P
                        op = mm3(b_up[:, n * TOK:(n + 1) * TOK], [w[:, e, f0:f0 + P] for w in w1_s], xnT_s)
                    op.then_inc(up_mm, 1)
                if y := expert_tile(T, s, front, 0):
                    i, e, t = y
                    if first and i == 0:
                        eng.wait_ge(load, 16 * N_LOADS)
                    eng.wait_ge(h_ready, T * SLOTS + (s - 1 if s % 2 else s))
                    if s == 0 and front:
                        eng.wait_ge(gexp_ready, T + 1)
                    if s == 1 and front:
                        eng.wait_ge(sel_ready, T + 1)
                    if s == 3:
                        eng.wait_ge(gateT_ready, T + 1)
                    if first and s == 2:
                        eng.wait_ge(sel_ready, T + 1)
                    else:
                        eng.wait_ge(y_used, i)
                    for ft in range(FT):
                        op = mm(b_misc[:, t * P:(t + 1) * P], hbuf[:, e % 2, ft, t * P:(t + 1) * P],
                                w2_s[:, e, ft], start=ft == 0, stop=ft == FT - 1)
                    op.then_inc(y_mm, 1)
                if front and odd:
                    eng.wait_ge(vT_ready, T * PAIRS + j + 1)
                    for t in range(TW):
                        eng.transpose(b_proj[:, 2 * t * P:(2 * t + 1) * P],
                                      qkT[:, j, 1, 2 * t:2 * t + 2].rearrange("p a b -> p (a b)"), id_s[:])
                        op = eng.transpose(b_proj[:, (2 * t + 1) * P:(2 * t + 2) * P],
                                           vT[:, j, t * P:(t + 1) * P], id_s[:])
                    op.then_inc(kv_mm, 1)
                if front and s == SLOTS - 1:
                    eng.wait_ge(h_ready, T * SLOTS + SLOTS)
                    eng.wait_ge(xn_ready, T + 2)
                    transpose_xn()
            slots(eng, slot)

        @block.vector
        def _(eng):
            def lo_part(lo, full, hi, scale=1.0):
                return eng.scalar_tensor_tensor(lo, full, scale, hi.bitcast(F32), ALU.mult, ALU.subtract)

            def mean_and_var(T):
                n = [0]

                def link(op):
                    n[0] += 1
                    op.then_inc(ln_chain, 1)
                    eng.wait_ge(ln_chain, T * LN_LINKS + n[0])
                eng.wait_ge(x_load, 32 * (T + 1))
                eng.bn_stats(stats[:, 0], x_s[:, 0])
                link(eng.bn_stats(stats[:, 1], x_s[:, 1]))
                eng.tensor_tensor(mean[:], stats[:, :, 1], stats[:, :, 4], ALU.add)
                eng.tensor_tensor(var_eps[:], stats[:, :, 2], stats[:, :, 5], ALU.add)
                link(eng.tensor_tensor(spread[:], stats[:, :, 1], stats[:, :, 4], ALU.subtract))
                eng.tensor_scalar(mean[:], mean[:], 0.5, None, ALU.mult)
                link(eng.tensor_tensor(spread[:], spread[:], spread[:], ALU.mult))
                link(eng.tensor_scalar(spread[:], spread[:], 0.25, LN_EPS, ALU.mult, ALU.add))
                eng.scalar_tensor_tensor(var_eps[:], var_eps[:], 1.0 / D, spread[:], ALU.mult, ALU.add)\
                    .then_inc(var_ready, 1)

            def normalise(T):
                n = [4]

                def link(op):
                    n[0] += 1
                    op.then_inc(ln_chain, 1)
                    eng.wait_ge(ln_chain, T * LN_LINKS + n[0])
                eng.wait_ge(rstd_guess, T + 1)
                link(eng.tensor_tensor(newton[:], rstd[:], rstd[:], ALU.mult))
                link(eng.tensor_tensor(newton[:], newton[:], var_eps[:], ALU.mult))
                link(eng.tensor_scalar(newton[:], newton[:], -0.5, 1.5, ALU.mult, ALU.add))
                link(eng.tensor_tensor(rstd[:], rstd[:], newton[:], ALU.mult))
                for t in range(TW):
                    op = eng.tensor_scalar(xn[:, t], x_s[:, t], mean[:, t:t + 1], rstd[:, t:t + 1],
                                           ALU.subtract, ALU.mult)
                op.then_inc(xn_ready, 1)
                assert n[0] == LN_LINKS

            def split_xnT(T):
                eng.wait_ge(xnT_copied, T + 1)
                lo_part(xnT_s[1][:], xnT[:], xnT_s[0][:]).then_inc(xnT_ready, 1)

            mean_and_var(0)
            for state in (w_io, w_outT):
                eng.memset(state[:], 0.0).then_inc(states_zero, 1)
            normalise(0)
            for n, (_, parts, scale) in enumerate(SPLIT):
                eng.wait_ge(hi_ready, n + 1)
                lo_part(parts[1], raw[:, n % RING], parts[0], scale).then_inc(lo_ready, 1)
            split_xnT(0)
            eng.wait_ge(load, 16 * N_LOADS)

            def gates(T):
                n = [0]

                def link(op):
                    n[0] += 1
                    op.then_inc(gate_chain, 1)
                    eng.wait_ge(gate_chain, T * GATE_LINKS + n[0])

                all4 = [P, TW, E, E]
                of_j, of_i = prob[:].unsqueeze(2).broadcast_to(all4), prob[:].unsqueeze(3).broadcast_to(all4)
                link(eng.reciprocal(grec[:], gsum[:]))
                link(eng.tensor_tensor(prob[:], gexp[:], grec[:].unsqueeze(2).broadcast_to([P, TW, E]), ALU.mult))
                link(eng.tensor_tensor(gt[:], of_j, of_i, ALU.is_gt))
                link(eng.tensor_tensor(eq[:], of_j, of_i, ALU.is_equal))
                link(eng.tensor_tensor(eq[:].rearrange("p t i j -> p t (i j)"), eq[:].rearrange("p t i j -> p t (i j)"),
                                       tri_s[:].unsqueeze(1).broadcast_to([P, TW, E * E]), ALU.mult))
                link(eng.tensor_tensor(gt[:], gt[:], eq[:], ALU.add))
                eng.tensor_reduce(cnt[:], gt[:], AX.X, ALU.add)
                link(eng.tensor_tensor(eq[:], gt[:], of_j, ALU.mult))
                link(eng.tensor_reduce(cum[:], eq[:], AX.X, ALU.add))
                link(eng.tensor_scalar(keep[:], cum[:], TOP_P, None, ALU.is_lt))
                link(eng.scalar_tensor_tensor(keep[:], cnt[:], 1.5, keep[:], ALU.is_lt, ALU.max))
                link(eng.tensor_tensor(gate[:], keep[:], prob[:], ALU.mult))
                assert n[0] == GATE_LINKS

            def slot(T, s, front, start, unit):
                first = is_first(T)
                j, odd = divmod(s, 2)
                if u := unit(0):
                    r, g = u
                    eng.wait_ge(z_mm, r + 1)
                    if not (first and g < 2):
                        eng.wait_ge(exp_ready, r - 1)
                    eng.tensor_reduce(nmax[:, g % 2], b_z[:, 0:4 * CHUNK].rearrange("p (a b) -> p a b", b=CHUNK),
                                      AX.X, ALU.max, negate=True).then_inc(max_ready, 1)
                if u := unit(2):
                    r, g = u
                    pair, twin = divmod(g, TW)
                    eng.wait_ge(grad_mm, r + 1)
                    eng.wait_ge(decayed, r + 1)
                    for h in range(2):
                        c = slice(h * CHUNK, (h + 1) * CHUNK)
                        blocks = w_io[c, :, pair, 2 * twin:2 * twin + 2, c]
                        grads = b_g[c, :, 0:2 * P].rearrange("p b (n c) -> p n b c", n=2)[:, :, :, c]
                        op = eng.tensor_tensor(blocks, blocks, grads, ALU.add)
                    op.then_inc(state_ready, 1)
                    if g == SLOTS - 1:
                        eng.wait_ge(attn_mm, r + 1)
                        eng.wait_ge(out_stored, 32 * (T - 1))
                        eng.tensor_tensor(out_s[:].rearrange("p t d -> p (t d)"), b_y[:, 0:TW * D],
                                          acc_done[:].rearrange("p t d -> p (t d)"), ALU.add).then_inc(out_ready, 1)
                if (u := unit(1)) and u[1] == 0:
                    if not first:
                        eng.wait_ge(decayed, u[0])
                    eng.tensor_copy(wd_rec[:].rearrange("p a b c -> p (a b) c"), wd_front[:]).then_inc(wd_ready, 1)
                if u := unit(0):
                    r, g = u
                    eng.wait_ge(exp_ready, r + 1)
                    if not (first and g < 2):
                        eng.wait_ge(p_ready, r - 1)
                    eng.reciprocal(erec[:, g % 2], esum[:, g % 2]).then_inc(erec_ready, 1)
                if y := expert_tile(T, s, front, 1):
                    i, e, t = y
                    eng.wait_ge(y_mm, i + 1)
                    eng.scalar_tensor_tensor((acc_done if e == E - 1 else acc)[:, t], b_misc[:, t * P:(t + 1) * P],
                                             gate[:, t, e:e + 1], (x_s if e == 0 else acc)[:, t],
                                             ALU.mult, ALU.add).then_inc(y_used, 1)
                if front and not odd:
                    eng.wait_ge(tanh_ready, T * PAIRS + j + 1)
                    if not first:
                        eng.wait_ge(z_mm, (T - 1) * SLOTS + 2 * j + 2)
                    eng.scalar_tensor_tensor(qkT[:, j].rearrange("p a b c -> p (a b c)"), tanh_s[:], 1.0, b_proj[:],
                                             ALU.add, ALU.mult).then_inc(qk_ready, 1)
                if u := unit(1):
                    r, g = u
                    eng.wait_ge(p_tok_ready, r + 1)
                    if not (first and g < 2):
                        eng.wait_ge(grad_mm, r - 1)
                    for h in range(2):
                        c = slice(h * CHUNK, (h + 1) * CHUNK)
                        op = eng.tensor_tensor_reduce(out=pa[:, c], in0=b_a[:, c], in1=p_tok[:, g % 2, c], scale=1.0,
                                                      scalar=0.0, op0=ALU.mult, op1=ALU.add,
                                                      accum_out=s_tok[:, h:h + 1])
                    op.then_inc(s_ready, 1)
                    eng.wait_ge(s_ready, r + 1)
                    for h in range(2):
                        c = slice(h * CHUNK, (h + 1) * CHUNK)
                        op = eng.scalar_tensor_tensor(g_tok[:, g % 2, c], b_a[:, c], s_tok[:, h:h + 1],
                                                      p_tok[:, g % 2, c], ALU.subtract, ALU.mult)
                    op.then_inc(g_ready, 1)
                if front and s == 0:
                    eng.wait_ge(logits_mm, T + 1)
                    eng.tensor_reduce(ngmax[:], b_misc[:, 0:TW * E].rearrange("p (a b) -> p a b", b=E), AX.X, ALU.max,
                                      negate=True).then_inc(gmax_ready, 1)
                    eng.wait_ge(lr_sum_ready, T + 1)
                    eng.tensor_scalar(lr_mean[:], lr_sum[:], 0.5 / CHUNK, 0.5, ALU.mult, ALU.add)\
                        .then_inc(lr_mean_ready, 1)
                    eng.wait_ge(lr_mean_ready, T + 1)
                    eng.tensor_tensor(wd_rhs[:], lr_mean[:].unsqueeze(1).broadcast_to([LR_ROWS, 2 * PAIRS, BG]),
                                      sel_wd_s[:].unsqueeze(2).broadcast_to([LR_ROWS, 2 * PAIRS, BG]), ALU.mult)
                    eng.tensor_copy(lr_wide[:].rearrange("r t (b n) -> r (t b) n", b=2),
                                    lr_mean[:].unsqueeze(2).broadcast_to([LR_ROWS, BG, CHUNK])).then_inc(lr_ready, 1)
                if front and s == 1:
                    eng.wait_ge(sel_mm, T + 1)
                    n = 2 * PAIRS * BG
                    eng.tensor_copy(wd_front[:].rearrange("p a b -> p (a b)"), b_misc[:, 0:n])
                    eng.tensor_copy(lr_tok[:].rearrange("p j t a b -> p t j (a b)"),
                                    b_misc[:, n:2 * n].rearrange("p (t j k) -> p t j k", t=TW, k=4))\
                        .then_inc(sel_ready, 1)
                if front and s == 2:
                    eng.wait_ge(gexp_ready, T + 1)
                    gates(T)
                if front and odd:
                    eng.wait_ge(kv_mm, T * PAIRS + j + 1)
                    if s == 1:
                        eng.wait_ge(sel_ready, T + 1)
                    if not first:
                        eng.wait_ge(grad_mm, (T - 1) * SLOTS + 2 * j + 2)
                    eng.tensor_tensor(kv[:, j].rearrange("p t a (h d) -> p (t a h) d", h=2),
                                      b_proj[:].rearrange("p (a d) -> p a d", d=CHUNK),
                                      lr_tok[:, j].rearrange("p t a b -> p (t a b)").unsqueeze(2)
                                      .broadcast_to([P, 8, CHUNK]), ALU.mult).then_inc(kv_ready, 1)
                if front and s == SLOTS - 4:
                    mean_and_var(T + 1)
                if front and s == SLOTS - 3:
                    eng.wait_ge(xnT_mm, T + 1)
                    normalise(T + 1)
                if front and s == SLOTS - 1:
                    split_xnT(T + 1)
            slots(eng, slot)


def kernel(**inputs):
    import numpy as np
    import concourse.bacc as _bacc
    from concourse import mybir as _mybir
    from concourse.bass_utils import run_bass_kernel_spmd as _run

    a = {k.split("_", 1)[1]: np.asarray(v) for k, v in inputs.items()}
    B, L, D = a["attn_x"].shape
    _, DI, H, DH = a["attn_W_in_init"].shape
    E, _, F = a["ffn_W1"].shape
    pairs = H // 2

    def by_pairs(w):
        return w.reshape(pairs, 2 * w.shape[1], w.shape[2]).transpose(1, 0, 2)

    w_in0 = a["attn_W_in_init"][0].transpose(1, 2, 0)
    w_out0 = a["attn_W_out_init"][0].transpose(1, 0, 2)
    rows = np.arange(4 * H)
    kind, head = rows // H, rows % H
    sel_half = (head[:, None] % 2 == np.arange(128)[None] // 64).astype(np.float32)
    cols = np.arange(2 * pairs)
    sel_wd = ((kind[:, None] == 2 + cols[None] // pairs) & (head[:, None] // 2 == cols[None] % pairs)) * np.float32(0.9)
    cols = np.arange(4 * pairs)
    sel_lr = ((head[:, None] == cols[None] // 4 * 2 + cols[None] % 2)
              & (kind[:, None] == cols[None] // 2 % 2)) * np.float32(0.001)
    tri = np.broadcast_to(np.tril(np.ones((E, E), np.float32)).reshape(1, -1), (128, E * E))
    arrays = {
        "x": a["attn_x"], "wqT": a["attn_Wq"].T, "wkT": a["attn_Wk"].T, "wvT": a["attn_Wv"].T,
        "wlbT": np.concatenate([a["attn_Wlr"], a["attn_Wbeta"]]).T,
        "woT": a["attn_Wo"].T.reshape(pairs, 128, D).transpose(1, 0, 2),
        "winT0": by_pairs(w_in0), "wout0": by_pairs(w_out0), "woutT0": by_pairs(w_out0.transpose(0, 2, 1)),
        "wr": a["ffn_Wr"], "br": a["ffn_br"][None], "w1": a["ffn_W1"],
        "b1T": a["ffn_b1"].reshape(E * F // 128, 128).T, "w2": a["ffn_W2"], "b2": a["ffn_b2"],
        "ident": np.eye(128, dtype=np.float32), "sel_half": sel_half, "sel_wd": sel_wd.astype(np.float32),
        "sel_lr": sel_lr.astype(np.float32), "tri": tri,
    }
    nc = _bacc.Bacc("TRN2", target_bir_lowering=False, num_devices=1)
    given = {f"in_{k}": np.ascontiguousarray(v) for k, v in arrays.items()}
    aps = {k: nc.dram_tensor(f"in_{k}", given[f"in_{k}"].shape, _mybir.dt.from_np(given[f"in_{k}"].dtype),
                             kind="ExternalInput").ap() for k in arrays}
    aps["out"] = nc.dram_tensor("out", (B, L, D), _mybir.dt.float32, kind="ExternalOutput").ap()
    build(nc, **aps)
    r = _run(nc, [given], core_ids=[0])
    return r.results[0]["out"]
```

```python
import concourse.bass as bass
from concourse import mybir
from concourse.alu_op_type import AluOpType as ALU
from contextlib import ExitStack

F32 = mybir.dt.float32
F32R = mybir.dt.float32r
ACT = mybir.ActivationFunctionType
AX = mybir.AxisListType

P = 128
CHUNK = 64
SLOTS = 16
LEAD = 4
LAST_LAG = 4
BASE_LR, BASE_WD = 0.001, 0.9
TOP_P = 0.8
LN_EPS = 1e-5


def build(nc, x, wqT, wkT, wvT, w1, w2, b2, front_pack, row_pack, state_pack, woT, out):
    B, L, D = x.shape
    HD = wqT.shape[1]
    PAIRS = HD // P
    E, _, F = w1.shape
    FT = F // P
    CHUNKS = L // CHUNK
    BG = 4
    GROUPS = B // BG
    TW = 2
    TOK = BG * CHUNK
    STEPS = GROUPS * CHUNKS
    LR_ROWS = row_pack.shape[0]
    RING = PAIRS
    assert D == P and HD == 2 * F and F == TW * 2 * P and PAIRS * TW == SLOTS and E * 2 == SLOTS and FT == 4

    ctx = ExitStack()
    with ctx:
        def sb(name, shape, dt=F32):
            return ctx.enter_context(nc.sbuf_tensor(name, shape, dt))

        def bank(name):
            return ctx.enter_context(nc.psum_tensor(name, [P, 512], F32))

        def sem(name):
            return ctx.enter_context(nc.semaphore(name))

        wq_s = [sb("wq_hi", [P, HD], F32R), sb("wq_lo", [P, HD], F32R)]
        wk_s = [sb("wk_hi", [P, HD], F32R), sb("wk_lo", [P, HD], F32R)]
        wv_s = [sb("wv_hi", [P, HD], F32R), sb("wv_lo", [P, HD], F32R)]
        wo_s = sb("wo_s", [P, PAIRS, D])
        state_init = sb("state_init", [P, 3, PAIRS, CHUNK])
        w1_s = [sb("w1_hi", [P, E, F], F32R), sb("w1_lo", [P, E, F], F32R)]
        w2_s = sb("w2_s", [P, E, FT, D])
        b2_s = sb("b2_s", [E, D])

        def columns(t, *widths):
            starts = [sum(widths[:i]) for i in range(len(widths))]
            assert sum(widths) == t.shape[1]
            return [t[:, o:o + w] for o, w in zip(starts, widths)]
        front_s = sb("front_s", list(front_pack.shape))
        id_s, wlog_s, br_s, b1_s, tri_s = columns(front_s, P, LR_ROWS + E, TW * E, E * FT, E * E)
        row_s = sb("row_s", list(row_pack.shape))
        sel_half_s, sel_wd_s, sel_lr_s = columns(row_s, P, 2 * PAIRS, 4 * PAIRS)
        x_s = sb("x_s", [P, TW, D])
        stats = sb("stats", [P, TW, 6])
        mean = sb("mean", [P, TW])
        spread = sb("spread", [P, TW])
        var_eps = sb("var_eps", [P, TW])
        minus_half = sb("minus_half", [P, TW])
        unused = sb("unused", [P, 1])
        rstd = sb("rstd", [P, TW])
        newton = sb("newton", [P, TW])
        xn = sb("xn", [P, TW, D])
        xnT = sb("xnT", [P, TOK])
        xnT_s = [sb("xnT_hi", [P, TOK], F32R), sb("xnT_lo", [P, TOK], F32R)]
        tanh_s = sb("tanh_s", [P, 2 * TOK])
        qkT = sb("qkT", [P, PAIRS, 2, BG, CHUNK])
        vT = sb("vT", [P, PAIRS, TOK])
        kv = sb("kv", [P, PAIRS, TW, 2, P])
        raw = kv[:].rearrange("p j t a d -> p j (t a d)")
        logits = sb("logits", [LR_ROWS + E, TOK])
        tanh_lr_s = sb("tanh_lr_s", [LR_ROWS, TOK])
        lr_sum = sb("lr_sum", [LR_ROWS, BG])
        lr_mean = sb("lr_mean", [LR_ROWS, BG])
        lr_wide = sb("lr_wide", [LR_ROWS, TW, P])
        wd_rhs = sb("wd_rhs", [LR_ROWS, 2 * PAIRS, BG])
        lr_tok = sb("lr_tok", [P, PAIRS, TW, 2, 2])
        wd_front = sb("wd_front", [P, 2 * PAIRS, BG])
        wd_rec = sb("wd_rec", [P, 2, PAIRS, BG])
        w_io = sb("w_io", [P, 2, PAIRS, BG, P])
        w_in = w_io[:, 0]
        w_out = w_io[:, 1]
        w_outT = sb("w_outT", [P, PAIRS, BG, P])
        nmax = sb("nmax", [P, 2, 4])
        ez = sb("ez", [P, 2, 4, CHUNK])
        esum = sb("esum", [P, 2, 4])
        erec = sb("erec", [P, 2, 4])
        pz = sb("pz", [P, 2, 4, CHUNK])
        p_tok = sb("p_tok", [P, 2, P])
        pa = sb("pa", [P, P])
        s_tok = sb("s_tok", [P, 2])
        g_tok = sb("g_tok", [P, 2, P])
        oT = sb("oT", [P, 2, P])
        hbuf = sb("hbuf", [P, 2, FT, TOK])
        router_logits = sb("router_logits", [P, TW, E])
        ngmax = sb("ngmax", [P, TW])
        gexp = sb("gexp", [P, TW, E])
        gsum = sb("gsum", [P, TW])
        grec = sb("grec", [P, TW])
        prob = sb("prob", [P, TW, E])
        gt = sb("gt", [P, TW, E, E])
        eq = sb("eq", [P, TW, E, E])
        cum = sb("cum", [P, TW, E])
        cnt = sb("cnt", [P, TW, E])
        keep = sb("keep", [P, TW, E])
        gate = sb("gate", [P, TW, E])
        gateT = sb("gateT", [E, TW * P])
        acc = sb("acc", [P, TW, D])
        acc_done = sb("acc_done", [P, TW, D])
        out_s = sb("out_s", [P, TW, D])

        b_proj = bank("b_proj")
        b_up = bank("b_up")
        b_misc = bank("b_misc")
        b_side = b_misc[:, 2 * P:4 * P]
        b_z = bank("b_z")
        b_a = bank("b_a")
        b_g = ctx.enter_context(nc.psum_tensor("b_g", [P, 2, 512], F32))
        b_y = bank("b_y")

        load = sem("load")
        load_states = sem("load_states")
        load_front = sem("load_front")
        raw_load = [sem(f"raw_load{i}") for i in range(RING)]
        hi_ready = sem("hi_ready")
        lo_ready = sem("lo_ready")
        x_load = sem("x_load")
        consts_set = sem("consts_set")
        states_zero = sem("states_zero")
        ln_chain = sem("ln_chain")
        rstd_guess = sem("rstd_guess")
        out_stored = sem("out_stored")
        xn_ready = sem("xn_ready")
        xnT_mm = sem("xnT_mm")
        xnT_copied = sem("xnT_copied")
        xnT_hi_ready = sem("xnT_hi_ready")
        xnT_ready = sem("xnT_ready")
        logits_mm = sem("logits_mm")
        logits_ready = sem("logits_ready")
        router_mm = sem("router_mm")
        router_ready = sem("router_ready")
        lr_sum_ready = sem("lr_sum_ready")
        lr_mean_ready = sem("lr_mean_ready")
        lr_ready = sem("lr_ready")
        gmax_ready = sem("gmax_ready")
        gexp_ready = sem("gexp_ready")
        gate_chain = sem("gate_chain")
        sel_mm = sem("sel_mm")
        sel_ready = sem("sel_ready")
        wd_ready = sem("wd_ready")
        gateT_mm = sem("gateT_mm")
        gateT_ready = sem("gateT_ready")
        out_ready = sem("out_ready")
        qk_mm = sem("qk_mm")
        tanh_ready = sem("tanh_ready")
        qk_ready = sem("qk_ready")
        v_mm = sem("v_mm")
        vT_ready = sem("vT_ready")
        kv_mm = sem("kv_mm")
        kv_ready = sem("kv_ready")
        y_mm = sem("y_mm")
        y_used = sem("y_used")
        up_mm = sem("up_mm")
        h_ready = sem("h_ready")
        z_mm = sem("z_mm")
        max_ready = sem("max_ready")
        exp_ready = sem("exp_ready")
        erec_ready = sem("erec_ready")
        p_ready = sem("p_ready")
        a_mm = sem("a_mm")
        p_tok_ready = sem("p_tok_ready")
        s_ready = sem("s_ready")
        decayed = sem("decayed")
        g_ready = sem("g_ready")
        attn_mm = sem("attn_mm")
        grad_mm = sem("grad_mm")
        state_ready = sem("state_ready")
        woutT_mm = sem("woutT_mm")
        woutT_ready = sem("woutT_ready")
        init_ready = sem("init_ready")

        N_LOADS, N_LOADS_FRONT = 3, 2
        INITS = 4
        GATE_LINKS = 10
        LN_LINKS = 9
        half_qkv = [[(w[:, c], [t[:, c] for t in parts], scale) for w, parts, scale in
                     ((wqT, wq_s, 0.5), (wkT, wk_s, 0.5), (wvT, wv_s, 1.0))] for c in (slice(0, F), slice(F, 2 * F))]
        w1_chunks = [(w1[e], [t[:, e] for t in w1_s], 1.0) for e in range(E)]
        SPLIT = half_qkv[0] + w1_chunks[:3] + half_qkv[1] + w1_chunks[3:]
        FIRST_SPLIT = 4
        QKV_SPLIT = {0: 3, PAIRS: 9}
        W1_SPLIT = [4, 5, 6, 10, 11, 12, 13, 14]

        def raw_place(n):
            half = RING // 2
            return (n + half) % RING if n < RING else half + n % half

        def raw_round(n):
            return sum(raw_place(m) == raw_place(n) for m in range(n + 1))

        def rows(a, group, c, half):
            b = group * BG + half
            return a[b:b + TW + 1:2, bass.ds(c * CHUNK, CHUNK), :].rearrange("w n d -> n w d")

        def is_first(T):
            return isinstance(T, int) and T == 0

        def expert_tile(T, s, front, lag):
            i = s - 2 - lag
            if (front and i >= 0) or (i < 0 and not is_first(T)):
                return (T * SLOTS + i, *divmod(i % SLOTS, TW))

        def slots(eng, slot):
            def step(T, s, front, lo, hi, start):
                def unit(lag):
                    r = s - LEAD - lag
                    return (T * SLOTS + r, r % SLOTS) if lo <= r < hi else None
                slot(T, s, front, start, unit)

            ALL = (-SLOTS - 8, SLOTS)
            for s in range(SLOTS):
                step(0, s, True, 0, SLOTS, True)
            with eng.Fori(1, CHUNKS) as T:
                for s in range(SLOTS):
                    step(T, s, True, *ALL, False)
            for g in range(1, GROUPS):
                for s in range(SLOTS):
                    step(g * CHUNKS, s, True, *ALL, True)
                with eng.Fori(g * CHUNKS + 1, (g + 1) * CHUNKS) as T:
                    for s in range(SLOTS):
                        step(T, s, True, *ALL, False)
            for s in range(LEAD + LAST_LAG):
                step(STEPS, s, False, -SLOTS, 0, False)

        block = ctx.enter_context(nc.Block())

        @block.sync
        def _(eng):
            def load_x(T, group, c):
                if not is_first(T):
                    eng.wait_ge(y_used, (T - 1) * SLOTS + 2)
                for half in range(2):
                    eng.dma_start(x_s[half * CHUNK:(half + 1) * CHUNK], rows(x, group, c, half)).then_inc(x_load, 16)

            def store(T, group, c):
                eng.wait_ge(out_ready, T + 1)
                for half in range(2):
                    eng.dma_start(rows(out, group, c, half), out_s[half * CHUNK:(half + 1) * CHUNK])\
                        .then_inc(out_stored, 16)

            def load_chunk(n):
                place = raw_place(n)
                if n >= RING:
                    before = max(m for m in range(n) if raw_place(m) == place)
                    eng.wait_ge(lo_ready, before + 1)
                eng.dma_start(raw[:, place], SPLIT[n][0]).then_inc(raw_load[place], 16)

            load_x(0, 0, 0)
            for n in range(RING):
                load_chunk(n)
            eng.dma_start(state_init[:], state_pack).then_inc(load_states, 16)
            for dst, src in ((w2_s[:], w2.rearrange("e (t f) d -> f e t d", f=P)),
                             (wo_s[:], woT), (b2_s[:], b2)):
                eng.dma_start(dst, src).then_inc(load, 16)
            for n in range(RING, len(SPLIT)):
                load_chunk(n)

            load_x(1, 0, 1)
            for group in range(GROUPS):
                T0 = group * CHUNKS
                if group:
                    load_x(T0, group, 0)
                    store(T0 - 2, group - 1, CHUNKS - 2)
                    load_x(T0 + 1, group, 1)
                    store(T0 - 1, group - 1, CHUNKS - 1)
                with eng.Fori(1, CHUNKS - 1) as c:
                    load_x(c + (T0 + 1), group, c + 1)
                    store(c + (T0 - 1), group, c - 1)
            load_x(STEPS, GROUPS - 1, CHUNKS - 1)
            store(STEPS - 2, GROUPS - 1, CHUNKS - 2)
            store(STEPS - 1, GROUPS - 1, CHUNKS - 1)
            eng.wait_ge(out_stored, 32 * (STEPS + 1))

        @block.gpsimd
        def _(eng):
            eng.memset(minus_half[:], -0.5).then_inc(consts_set, 1)
            eng.memset(unused[:], 0.0).then_inc(out_stored, 32)
            eng.wait_ge(consts_set, 1)
            eng.memset(w_outT[:], 0.0).then_inc(states_zero, 1)

            def guess_rstd(T):
                eng.wait_ge(ln_chain, T * LN_LINKS + 5)
                eng.tensor_tensor(rstd[:], var_eps[:], minus_half[:], ALU.pow).then_inc(rstd_guess, 1)

            guess_rstd(0)
            eng.wait_ge(rstd_guess, 1)
            eng.memset(w_io[:], 0.0).then_inc(states_zero, 1)
            eng.wait_ge(load_states, 16)
            eng.wait_ge(states_zero, 2)

            def start_states(T, g):
                pair, twin = divmod(g, TW)
                if T > 0:
                    eng.wait_ge(woutT_ready, (T - 1) * SLOTS + g + 1)
                bs = slice(2 * twin, 2 * twin + 2)
                for h in range(2):
                    c = slice(h * CHUNK, (h + 1) * CHUNK)
                    src = state_init[c, :, pair].unsqueeze(2).broadcast_to([CHUNK, 3, 2, CHUNK])
                    eng.tensor_copy(w_io[c, :, pair, bs, c], src[:, 0:2]).then_inc(init_ready, 1)
                    eng.tensor_copy(w_outT[c, pair, bs, c], src[:, 2]).then_inc(init_ready, 1)

            def slot(T, s, front, start, unit):
                if start:
                    done = min(s + 2, SLOTS)
                    if T * SLOTS + s > LEAD:
                        eng.wait_ge(decayed, T * SLOTS + s - LEAD - 1)
                        eng.wait_ge(p_ready, T * SLOTS + s - LEAD)
                    if s == 8:
                        eng.wait_ge(rstd_guess, T + 2)
                    for g in range(s + 1 if s else 0, done):
                        start_states(T, g)
                    eng.wait_ge(init_ready, (T // CHUNKS * SLOTS + done) * INITS)
                if u := unit(0):
                    r, g = u
                    eng.wait_ge(erec_ready, r + 1)
                    if not (is_first(T) and g < 2):
                        eng.wait_ge(a_mm, r - 1)
                    eng.tensor_tensor(pz[:, g % 2], ez[:, g % 2],
                                      erec[:, g % 2].unsqueeze(2).broadcast_to([P, 4, CHUNK]),
                                      ALU.mult).then_inc(p_ready, 1)
                if u := unit(1):
                    r, g = u
                    pair, twin = divmod(g, TW)
                    bs = slice(2 * twin, 2 * twin + 2)
                    if g == 0:
                        eng.wait_ge(wd_ready, T + 1)
                    eng.wait_ge(a_mm, r + 1)
                    eng.tensor_tensor(w_io[:, :, pair, bs], w_io[:, :, pair, bs],
                                      wd_rec[:, :, pair, bs].unsqueeze(3).broadcast_to([P, 2, 2, P]),
                                      ALU.mult).then_inc(decayed, 1)
                if front and s == 7:
                    guess_rstd(T + 1)
            slots(eng, slot)

        @block.scalar
        def _(eng):
            def split_xnT(T):
                eng.wait_ge(xnT_copied, T + 1)
                eng.activation(xnT_s[0][:], xnT[:], ACT.Copy).then_inc(xnT_hi_ready, 1)

            def tanh_lr(T):
                eng.wait_ge(logits_ready, T + 1)
                if not is_first(T):
                    eng.wait_ge(lr_mean_ready, T)
                for b in range(BG):
                    c = slice(b * CHUNK, (b + 1) * CHUNK)
                    op = eng.activation(tanh_lr_s[:, c], logits[0:LR_ROWS, c], ACT.Tanh,
                                        scale=0.5, accum_out=lr_sum[:, b:b + 1])
                op.then_inc(lr_sum_ready, 1)

            def exp_router(T):
                eng.wait_ge(gmax_ready, T + 1)
                for t in range(TW):
                    op = eng.activation(gexp[:, t], router_logits[:, t], ACT.Exp,
                                        bias=ngmax[:, t:t + 1], accum_out=gsum[:, t:t + 1])
                op.then_inc(gexp_ready, 1)

            for dst, src in ((front_s, front_pack), (row_s, row_pack)):
                eng.dma_start(dst[:], src).then_inc(load_front, 16)
            split_xnT(0)
            tanh_lr(0)
            exp_router(0)

            def split_weights(n):
                _, parts, scale = SPLIT[n]
                eng.wait_ge(raw_load[raw_place(n)], 16 * raw_round(n))
                eng.activation(parts[0], raw[:, raw_place(n)], ACT.Copy, scale=scale).then_inc(hi_ready, 1)

            for n in range(FIRST_SPLIT):
                split_weights(n)

            def slot(T, s, front, start, unit):
                first = is_first(T)
                j, odd = divmod(s, 2)
                if first and s < len(SPLIT) - FIRST_SPLIT:
                    split_weights(FIRST_SPLIT + s)
                if u := unit(0):
                    r, g = u
                    eng.wait_ge(max_ready, r + 1)
                    if not (first and g < 2):
                        eng.wait_ge(p_ready, r - 1)
                    for n in range(4):
                        op = eng.activation(ez[:, g % 2, n], b_z[:, n * CHUNK:(n + 1) * CHUNK], ACT.Exp,
                                            bias=nmax[:, g % 2, n:n + 1], accum_out=esum[:, g % 2, n:n + 1])
                    op.then_inc(exp_ready, 1)
                if u := unit(LAST_LAG):
                    r, g = u
                    pair, twin = divmod(g, TW)
                    eng.wait_ge(woutT_mm, r + 1)
                    eng.activation(w_outT[:, pair, 2 * twin:2 * twin + 2], b_z[:, 2 * P:4 * P], ACT.Copy)\
                        .then_inc(woutT_ready, 1)
                if u := unit(1):
                    r, g = u
                    eng.wait_ge(a_mm, r + 1)
                    if not (first and g < 2):
                        eng.wait_ge(grad_mm, r - 1)
                        eng.wait_ge(attn_mm, r - 1)
                    eng.activation(p_tok[:, g % 2], b_a[:, P:2 * P], ACT.Copy)
                    eng.activation(oT[:, g % 2], b_a[:, 2 * P:3 * P], ACT.Copy).then_inc(p_tok_ready, 1)
                if front and not odd:
                    eng.wait_ge(qk_mm, T * PAIRS + j + 1)
                    if not (first and s == 0):
                        eng.wait_ge(qk_ready, T * PAIRS + j)
                    eng.activation(tanh_s[:], b_proj[:], ACT.Tanh).then_inc(tanh_ready, 1)
                if front and odd:
                    eng.wait_ge(v_mm, T * PAIRS + j + 1)
                    eng.activation(vT[:, j], b_proj[:, 0:TOK], ACT.Copy).then_inc(vT_ready, 1)
                if front:
                    e = j
                    eng.wait_ge(up_mm, T * SLOTS + s + 1)
                    if s == SLOTS - 1:
                        split_xnT(T + 1)
                    if not (first and e < 2):
                        eng.wait_ge(y_mm, T * SLOTS + 2 * e - 2)
                    for n in range(2):
                        ft = 2 * odd + n
                        op = eng.activation(hbuf[:, e % 2, ft], b_up[:, n * TOK:(n + 1) * TOK], ACT.Relu,
                                            bias=b1_s[:, e * FT + ft:e * FT + ft + 1])
                    op.then_inc(h_ready, 1)
                if front and s == SLOTS - 3:
                    tanh_lr(T + 1)
                if front and s == SLOTS - 1:
                    exp_router(T + 1)
            slots(eng, slot)

        @block.tensor
        def _(eng):
            def mm(o, a, b, start=True, stop=True, **kw):
                return eng.matmul(o, a, b, start=start, stop=stop, **kw)

            def transpose_xn(T):
                eng.wait_ge(xn_ready, T + 1)
                if not is_first(T):
                    eng.wait_ge(gateT_ready, T)
                for t in range(TW):
                    op = eng.transpose(b_side[:, t * P:(t + 1) * P], xn[:, t], id_s)
                op.then_inc(xnT_mm, 1)

            def logits_product(T):
                eng.wait_ge(xnT_copied, T + 1)
                mm(b_side[0:LR_ROWS + E], wlog_s, xnT[:]).then_inc(logits_mm, 1)

            def transpose_router(T):
                eng.wait_ge(logits_ready, T + 1)
                n = LR_ROWS + E
                for t in range(TW):
                    op = eng.transpose(b_side[:, t * n:(t + 1) * n], logits[:, t * P:(t + 1) * P], id_s[0:n, 0:n])
                op.then_inc(router_mm, 1)

            def mm3(o, a, b):
                mm(o, a[0], b[0][:], stop=False)
                mm(o, a[0], b[1][:], start=False, stop=False)
                return mm(o, a[1], b[0][:], start=False)

            eng.wait_ge(load_front, 16 * N_LOADS_FRONT)
            transpose_xn(0)
            logits_product(0)
            transpose_router(0)

            def slot(T, s, front, start, unit):
                first = is_first(T)
                j, odd = divmod(s, 2)
                e = j
                if first and s in QKV_SPLIT:
                    eng.wait_ge(lo_ready, QKV_SPLIT[s])
                if u := unit(LAST_LAG):
                    r, g = u
                    pair, twin = divmod(g, TW)
                    eng.wait_ge(state_ready, r + 1)
                    eng.wait_ge(exp_ready, r + LAST_LAG if unit(0) else T * SLOTS)
                    if not (first and g == 0):
                        eng.wait_ge(woutT_ready, r)
                    for b in range(2):
                        op = eng.transpose(b_z[:, (2 + b) * P:(3 + b) * P], w_out[:, pair, 2 * twin + b], id_s)
                    op.then_inc(woutT_mm, 1)
                if u := unit(0):
                    r, g = u
                    pair, twin = divmod(g, TW)
                    if start and s >= LEAD:
                        eng.wait_ge(init_ready, (T // CHUNKS * SLOTS + g + 1) * INITS)
                    if not (first and g == 0):
                        eng.wait_ge(exp_ready, r)
                    for b in range(2):
                        op = mm(b_z[:, 0:4 * CHUNK].rearrange("p (a b n) -> p a b n", a=2, b=2)[:, :, b],
                                w_in[:, pair, 2 * twin + b], qkT[:, pair, :, 2 * twin + b])
                    op.then_inc(z_mm, 1)
                if front and start and s == SLOTS - 1:
                    eng.wait_ge(init_ready, (T // CHUNKS + 1) * SLOTS * INITS)
                if u := unit(2):
                    r, g = u
                    pair, twin = divmod(g, TW)
                    if g == 0:
                        eng.wait_ge(gateT_ready, T + 1)
                        if not first:
                            eng.wait_ge(out_ready, T)
                        mm(b_y[:, 0:P], gateT[:, 0:P], b2_s[:], stop=False, skip_group_check=True)
                        mm(b_y[:, P:2 * P], gateT[:, P:2 * P], b2_s[:], start=False, stop=False, skip_group_check=True)
                    eng.wait_ge(p_tok_ready, r + 1)
                    eng.wait_ge(g_ready, r + 1)
                    if not (first and g == 0):
                        eng.wait_ge(state_ready, r)
                    mm(b_y[:, twin * P:(twin + 1) * P], oT[:, g % 2], wo_s[:, pair], start=False,
                       stop=pair == PAIRS - 1, skip_group_check=True).then_inc(attn_mm, 1)
                    for io in range(2):
                        for b in range(2):
                            n = slice(b * CHUNK, (b + 1) * CHUNK)
                            k, v, p, dz = kv[n, pair, twin, 0], kv[n, pair, twin, 1], p_tok[n, g % 2], g_tok[n, g % 2]
                            lhs, rhs = (p, v) if io else (k, dz)
                            for h in range(2):
                                c = slice(h * CHUNK, (h + 1) * CHUNK)
                                op = mm(b_g[c, b, io * P + h * CHUNK:io * P + (h + 1) * CHUNK], lhs[:, c], rhs[:, c])
                    op.then_inc(grad_mm, 1)
                if u := unit(1):
                    r, g = u
                    pair, twin = divmod(g, TW)
                    if not (first and g == 0):
                        eng.wait_ge(g_ready, r)
                    for b in range(2):
                        n0 = twin * P + b * CHUNK
                        mm(b_a[b * CHUNK:(b + 1) * CHUNK, 0:P], vT[:, pair, n0:n0 + CHUNK],
                           w_outT[:, pair, 2 * twin + b])
                    eng.wait_ge(p_ready, r + 1)
                    for b in range(2):
                        for h in range(2):
                            c = slice(h * CHUNK, (h + 1) * CHUNK)
                            mm(b_a[c, 2 * P + b * CHUNK:2 * P + (b + 1) * CHUNK], w_out[:, pair, 2 * twin + b, c],
                               pz[:, g % 2, b])
                    eng.transpose(b_a[:, P:2 * P], pz[:, g % 2, 2:4].rearrange("p a b -> p (a b)"), id_s)\
                        .then_inc(a_mm, 1)
                if front and not odd:
                    if s == 0:
                        eng.wait_ge(xnT_ready, T + 1)
                    if not (first and s == 0):
                        eng.wait_ge(kv_ready, T * PAIRS + j)
                    c = slice(j * P, (j + 1) * P)
                    mm3(b_proj[:, 0:TOK], [w[:, c] for w in wq_s], xnT_s)
                    mm3(b_proj[:, TOK:2 * TOK], [w[:, c] for w in wk_s], xnT_s).then_inc(qk_mm, 1)
                if front and odd:
                    eng.wait_ge(qk_ready, T * PAIRS + j + 1)
                    c = slice(j * P, (j + 1) * P)
                    mm3(b_proj[:, 0:TOK], [w[:, c] for w in wv_s], xnT_s).then_inc(v_mm, 1)
                if front:
                    if first and not odd:
                        eng.wait_ge(lo_ready, W1_SPLIT[e])
                    if not (first and s == 0):
                        eng.wait_ge(h_ready, T * SLOTS + s)
                    for n in range(2):
                        f0 = (2 * odd + n) * P
                        op = mm3(b_up[:, n * TOK:(n + 1) * TOK], [w[:, e, f0:f0 + P] for w in w1_s], xnT_s)
                    op.then_inc(up_mm, 1)
                y = expert_tile(T, s, front, 0)
                if y and not (first and s == 2):
                    eng.wait_ge(y_used, y[0])
                if front and s == 0:
                    eng.wait_ge(gmax_ready, T + 1)
                    eng.wait_ge(lr_ready, T + 1)
                    n = 2 * PAIRS * BG
                    mm(b_side[:, 0:n], sel_half_s, wd_rhs[:].rearrange("r a b -> r (a b)"))
                    for t in range(TW):
                        op = mm(b_side[:, n + t * 4 * PAIRS:n + (t + 1) * 4 * PAIRS], lr_wide[:, t], sel_lr_s)
                    op.then_inc(sel_mm, 1)
                if front and s == 4:
                    eng.wait_ge(gate_chain, (T + 1) * GATE_LINKS)
                    eng.wait_ge(sel_ready, T + 1)
                    for t in range(TW):
                        op = eng.transpose(b_side[0:E, t * P:(t + 1) * P], gate[:, t], id_s)
                    op.then_inc(gateT_mm, 1)
                if front and s == 10:
                    transpose_xn(T + 1)
                if front and s == 12:
                    logits_product(T + 1)
                if front and s == 14:
                    transpose_router(T + 1)
                if y:
                    i, e, t = y
                    if first and i == 0:
                        eng.wait_ge(load, 16 * N_LOADS)
                        eng.wait_ge(sel_ready, T + 1)
                    eng.wait_ge(h_ready, T * SLOTS + (s - 1 if s % 2 else s))
                    for ft in range(FT):
                        op = mm(b_misc[:, t * P:(t + 1) * P], hbuf[:, e % 2, ft, t * P:(t + 1) * P],
                                w2_s[:, e, ft], start=ft == 0, stop=ft == FT - 1)
                    op.then_inc(y_mm, 1)
                if front and odd:
                    eng.wait_ge(vT_ready, T * PAIRS + j + 1)
                    for t in range(TW):
                        eng.transpose(b_proj[:, 2 * t * P:(2 * t + 1) * P],
                                      qkT[:, j, 1, 2 * t:2 * t + 2].rearrange("p a b -> p (a b)"), id_s)
                        op = eng.transpose(b_proj[:, (2 * t + 1) * P:(2 * t + 2) * P],
                                           vT[:, j, t * P:(t + 1) * P], id_s)
                    op.then_inc(kv_mm, 1)
            slots(eng, slot)

        @block.vector
        def _(eng):
            def lo_part(lo, full, hi, scale=1.0):
                return eng.scalar_tensor_tensor(lo, full, scale, hi.bitcast(F32), ALU.mult, ALU.subtract)

            def layernorm(T, n):
                if n == 0:
                    eng.wait_ge(x_load, 32 * (T + 1))
                elif n == 5:
                    eng.wait_ge(rstd_guess, T + 1)
                else:
                    eng.wait_ge(ln_chain, T * LN_LINKS + n)
                if n == 0:
                    eng.bn_stats(stats[:, 0], x_s[:, 0])
                    op = eng.bn_stats(stats[:, 1], x_s[:, 1])
                if n == 1:
                    eng.tensor_tensor(mean[:], stats[:, :, 1], stats[:, :, 4], ALU.add)
                    eng.tensor_tensor(var_eps[:], stats[:, :, 2], stats[:, :, 5], ALU.add)
                    op = eng.tensor_tensor(spread[:], stats[:, :, 1], stats[:, :, 4], ALU.subtract)
                if n == 2:
                    eng.tensor_scalar(mean[:], mean[:], 0.5, None, ALU.mult)
                    op = eng.tensor_tensor(spread[:], spread[:], spread[:], ALU.mult)
                if n == 3:
                    op = eng.tensor_scalar(spread[:], spread[:], 0.25, LN_EPS, ALU.mult, ALU.add)
                if n == 4:
                    op = eng.scalar_tensor_tensor(var_eps[:], var_eps[:], 1.0 / D, spread[:], ALU.mult, ALU.add)
                if n == 5:
                    op = eng.tensor_tensor(newton[:], rstd[:], rstd[:], ALU.mult)
                if n == 6:
                    op = eng.tensor_tensor(newton[:], newton[:], var_eps[:], ALU.mult)
                if n == 7:
                    op = eng.tensor_scalar(newton[:], newton[:], -0.5, 1.5, ALU.mult, ALU.add)
                if n == 8:
                    op = eng.tensor_tensor(rstd[:], rstd[:], newton[:], ALU.mult)
                if n < LN_LINKS:
                    op.then_inc(ln_chain, 1)
                else:
                    for t in range(TW):
                        op = eng.tensor_scalar(xn[:, t], x_s[:, t], mean[:, t:t + 1], rstd[:, t:t + 1],
                                               ALU.subtract, ALU.mult)
                    op.then_inc(xn_ready, 1)

            def copy_xnT(T):
                eng.wait_ge(xnT_mm, T + 1)
                eng.tensor_copy(xnT[:], b_side[:]).then_inc(xnT_copied, 1)

            def split_xnT(T):
                eng.wait_ge(xnT_hi_ready, T + 1)
                lo_part(xnT_s[1][:], xnT[:], xnT_s[0][:]).then_inc(xnT_ready, 1)

            def copy_logits(T):
                eng.wait_ge(logits_mm, T + 1)
                eng.tensor_copy(logits[:], b_side[0:LR_ROWS + E]).then_inc(logits_ready, 1)

            def copy_router_logits(T):
                eng.wait_ge(router_mm, T + 1)
                logits_tok = b_side[:, 0:TW * (LR_ROWS + E)].rearrange("p (t n) -> p t n", t=TW)
                eng.tensor_tensor(router_logits[:], logits_tok[:, :, LR_ROWS:LR_ROWS + E],
                                  br_s.rearrange("p (t e) -> p t e", t=TW), ALU.add).then_inc(router_ready, 1)

            def max_router(T):
                eng.wait_ge(router_ready, T + 1)
                eng.tensor_reduce(ngmax[:], router_logits[:], AX.X, ALU.max, negate=True).then_inc(gmax_ready, 1)

            def spread_rates(T):
                eng.wait_ge(lr_sum_ready, T + 1)
                eng.tensor_scalar(lr_mean[:], lr_sum[:], 0.5 / CHUNK, 0.5, ALU.mult, ALU.add)\
                    .then_inc(lr_mean_ready, 1)
                eng.wait_ge(lr_mean_ready, T + 1)
                eng.tensor_tensor(wd_rhs[:], lr_mean[:].unsqueeze(1).broadcast_to([LR_ROWS, 2 * PAIRS, BG]),
                                  sel_wd_s.unsqueeze(2).broadcast_to([LR_ROWS, 2 * PAIRS, BG]), ALU.mult)
                eng.tensor_copy(lr_wide[:].rearrange("r t (b n) -> r (t b) n", b=2),
                                lr_mean[:].unsqueeze(2).broadcast_to([LR_ROWS, BG, CHUNK])).then_inc(lr_ready, 1)

            for n in range(LN_LINKS + 1):
                layernorm(0, n)
            copy_xnT(0)
            split_xnT(0)
            copy_logits(0)
            eng.wait_ge(load_front, 16 * N_LOADS_FRONT)
            copy_router_logits(0)
            max_router(0)
            spread_rates(0)

            def split_weights(n):
                _, parts, scale = SPLIT[n]
                eng.wait_ge(hi_ready, n + 1)
                lo_part(parts[1], raw[:, raw_place(n)], parts[0], scale).then_inc(lo_ready, 1)

            for n in range(FIRST_SPLIT):
                split_weights(n)

            def gates(T, n):
                if n == 0:
                    eng.wait_ge(gexp_ready, T + 1)
                else:
                    eng.wait_ge(gate_chain, T * GATE_LINKS + n)
                all4 = [P, TW, E, E]
                of_j, of_i = prob[:].unsqueeze(2).broadcast_to(all4), prob[:].unsqueeze(3).broadcast_to(all4)
                if n == 0:
                    op = eng.reciprocal(grec[:], gsum[:])
                if n == 1:
                    op = eng.tensor_tensor(prob[:], gexp[:], grec[:].unsqueeze(2).broadcast_to([P, TW, E]), ALU.mult)
                if n == 2:
                    eng.tensor_tensor(gt[:], of_j, of_i, ALU.is_gt)
                    op = eng.tensor_tensor(eq[:], of_j, of_i, ALU.is_equal)
                if n == 3:
                    op = eng.tensor_tensor(eq[:].rearrange("p t i j -> p t (i j)"),
                                           eq[:].rearrange("p t i j -> p t (i j)"),
                                           tri_s.unsqueeze(1).broadcast_to([P, TW, E * E]), ALU.mult)
                if n == 4:
                    op = eng.tensor_tensor(gt[:], gt[:], eq[:], ALU.add)
                if n == 5:
                    eng.tensor_reduce(cnt[:], gt[:], AX.X, ALU.add)
                    op = eng.tensor_tensor(eq[:], gt[:], of_j, ALU.mult)
                if n == 6:
                    op = eng.tensor_reduce(cum[:], eq[:], AX.X, ALU.add)
                if n == 7:
                    op = eng.tensor_scalar(keep[:], cum[:], TOP_P, None, ALU.is_lt)
                if n == 8:
                    op = eng.scalar_tensor_tensor(keep[:], cnt[:], 1.5, keep[:], ALU.is_lt, ALU.max)
                if n == 9:
                    op = eng.tensor_tensor(gate[:], keep[:], prob[:], ALU.mult)
                op.then_inc(gate_chain, 1)

            def chains(T, s, place):
                if s < 3:
                    n = 3 * s + place
                    gates(T, n)
                    if n == GATE_LINKS - 2:
                        gates(T, n + 1)
                        eng.wait_ge(gate_chain, (T + 1) * GATE_LINKS)
                if 3 * 6 <= 3 * s + place < 3 * 6 + 5:
                    layernorm(T + 1, 3 * (s - 6) + place)
                if 3 * 8 + 2 <= 3 * s + place <= 3 * 10:
                    layernorm(T + 1, 3 * (s - 7) + place)

            def slot(T, s, front, start, unit):
                first = is_first(T)
                j, odd = divmod(s, 2)
                if u := unit(0):
                    r, g = u
                    eng.wait_ge(z_mm, r + 1)
                    if not (first and g < 2):
                        eng.wait_ge(exp_ready, r - 1)
                    eng.tensor_reduce(nmax[:, g % 2], b_z[:, 0:4 * CHUNK].rearrange("p (a b) -> p a b", b=CHUNK),
                                      AX.X, ALU.max, negate=True).then_inc(max_ready, 1)
                y = expert_tile(T, s, front, 1)
                if y:
                    eng.wait_ge(y_mm, y[0] + 1)
                if front and s == 1:
                    eng.wait_ge(sel_mm, T + 1)
                    n = 2 * PAIRS * BG
                    eng.tensor_copy(wd_front[:].rearrange("p a b -> p (a b)"), b_side[:, 0:n])
                    eng.tensor_copy(lr_tok[:].rearrange("p j t a b -> p t j (a b)"),
                                    b_side[:, n:2 * n].rearrange("p (t j k) -> p t j k", t=TW, k=4))\
                        .then_inc(sel_ready, 1)
                if front and s == 5:
                    eng.wait_ge(gateT_mm, T + 1)
                    eng.tensor_copy(gateT[:], b_side[0:E]).then_inc(gateT_ready, 1)
                if front and s == 11:
                    copy_xnT(T + 1)
                if front and s == 13:
                    copy_logits(T + 1)
                if front and s == 15:
                    copy_router_logits(T + 1)
                if y:
                    i, e, t = y
                    eng.scalar_tensor_tensor((acc_done if e == E - 1 else acc)[:, t], b_misc[:, t * P:(t + 1) * P],
                                             gate[:, t, e:e + 1], (x_s if e == 0 else acc)[:, t],
                                             ALU.mult, ALU.add).then_inc(y_used, 1)
                if u := unit(2):
                    r, g = u
                    pair, twin = divmod(g, TW)
                    eng.wait_ge(grad_mm, r + 1)
                    eng.wait_ge(decayed, r + 1)
                    for h in range(2):
                        c = slice(h * CHUNK, (h + 1) * CHUNK)
                        blocks = w_io[c, :, pair, 2 * twin:2 * twin + 2, c]
                        grads = b_g[c, :, 0:2 * P].rearrange("p b (n c) -> p n b c", n=2)[:, :, :, c]
                        op = eng.tensor_tensor(blocks, blocks, grads, ALU.add)
                    op.then_inc(state_ready, 1)
                    if g == SLOTS - 1:
                        eng.wait_ge(attn_mm, r + 1)
                        eng.wait_ge(out_stored, 32 * T)
                        eng.tensor_tensor(out_s[:].rearrange("p t d -> p (t d)"), b_y[:, 0:TW * D],
                                          acc_done[:].rearrange("p t d -> p (t d)"), ALU.add).then_inc(out_ready, 1)
                if (u := unit(1)) and u[1] == 0:
                    if not first:
                        eng.wait_ge(decayed, u[0])
                    eng.tensor_copy(wd_rec[:].rearrange("p a b c -> p (a b) c"), wd_front[:]).then_inc(wd_ready, 1)
                if front:
                    chains(T, s, 0)
                if u := unit(0):
                    r, g = u
                    eng.wait_ge(exp_ready, r + 1)
                    if not (first and g < 2):
                        eng.wait_ge(p_ready, r - 1)
                    eng.reciprocal(erec[:, g % 2], esum[:, g % 2]).then_inc(erec_ready, 1)
                if front:
                    chains(T, s, 1)
                if u := unit(1):
                    r, g = u
                    eng.wait_ge(p_tok_ready, r + 1)
                    if not (first and g < 2):
                        eng.wait_ge(grad_mm, r - 1)
                    for h in range(2):
                        c = slice(h * CHUNK, (h + 1) * CHUNK)
                        op = eng.tensor_tensor_reduce(out=pa[:, c], in0=b_a[:, c], in1=p_tok[:, g % 2, c], scale=1.0,
                                                      scalar=0.0, op0=ALU.mult, op1=ALU.add,
                                                      accum_out=s_tok[:, h:h + 1])
                    op.then_inc(s_ready, 1)
                    eng.wait_ge(s_ready, r + 1)
                    for h in range(2):
                        c = slice(h * CHUNK, (h + 1) * CHUNK)
                        op = eng.scalar_tensor_tensor(g_tok[:, g % 2, c], b_a[:, c], s_tok[:, h:h + 1],
                                                      p_tok[:, g % 2, c], ALU.subtract, ALU.mult)
                    op.then_inc(g_ready, 1)
                if front and not odd:
                    eng.wait_ge(tanh_ready, T * PAIRS + j + 1)
                    if not first:
                        eng.wait_ge(z_mm, (T - 1) * SLOTS + 2 * j + 2)
                    eng.scalar_tensor_tensor(qkT[:, j].rearrange("p a b c -> p (a b c)"), tanh_s[:], 1.0, b_proj[:],
                                             ALU.add, ALU.mult).then_inc(qk_ready, 1)
                if front:
                    chains(T, s, 2)
                if first and s < len(SPLIT) - FIRST_SPLIT:
                    split_weights(FIRST_SPLIT + s)
                if front and s == 14:
                    spread_rates(T + 1)
                if front and s == 15:
                    max_router(T + 1)
                    split_xnT(T + 1)
                if front and odd:
                    eng.wait_ge(kv_mm, T * PAIRS + j + 1)
                    if s == 1:
                        eng.wait_ge(sel_ready, T + 1)
                    if not first:
                        eng.wait_ge(grad_mm, (T - 1) * SLOTS + 2 * j + 2)
                    eng.tensor_tensor(kv[:, j].rearrange("p t a (h d) -> p (t a h) d", h=2),
                                      b_proj[:].rearrange("p (a d) -> p a d", d=CHUNK),
                                      lr_tok[:, j].rearrange("p t a b -> p (t a b)").unsqueeze(2)
                                      .broadcast_to([P, 8, CHUNK]), ALU.mult).then_inc(kv_ready, 1)
            slots(eng, slot)


def kernel(**inputs):
    import numpy as np
    import concourse.bacc as _bacc
    from concourse import mybir as _mybir
    from concourse.bass_utils import run_bass_kernel_spmd as _run

    a = {k.split("_", 1)[1]: np.asarray(v) for k, v in inputs.items()}
    B, L, D = a["attn_x"].shape
    _, DI, H, DH = a["attn_W_in_init"].shape
    E, _, F = a["ffn_W1"].shape
    pairs = H // 2

    def by_pairs(w):
        return w.reshape(pairs, 2 * w.shape[1], w.shape[2]).transpose(1, 0, 2)

    w_in0 = a["attn_W_in_init"][0].transpose(1, 2, 0)
    w_out0 = a["attn_W_out_init"][0].transpose(1, 0, 2)
    rows = np.arange(4 * H)
    kind, head = rows // H, rows % H
    sel_half = (head[:, None] % 2 == np.arange(128)[None] // 64).astype(np.float32)
    cols = np.arange(2 * pairs)
    sel_wd = ((kind[:, None] == 2 + cols[None] // pairs) & (head[:, None] // 2 == cols[None] % pairs)) * np.float32(0.9)
    cols = np.arange(4 * pairs)
    sel_lr = ((head[:, None] == cols[None] // 4 * 2 + cols[None] % 2)
              & (kind[:, None] == cols[None] // 2 % 2)) * np.float32(0.001)
    tri = np.broadcast_to(np.tril(np.ones((E, E), np.float32)).reshape(1, -1), (128, E * E))
    b1 = a["ffn_b1"].reshape(E * F // 128, 128).T
    router_bias = np.broadcast_to(np.tile(a["ffn_br"], 2), (128, 2 * E))
    arrays = {
        "x": a["attn_x"], "wqT": a["attn_Wq"].T, "wkT": a["attn_Wk"].T, "wvT": a["attn_Wv"].T,
        "w1": a["ffn_W1"], "w2": a["ffn_W2"], "b2": a["ffn_b2"],
        "front_pack": np.concatenate([np.eye(128, dtype=np.float32), a["attn_Wlr"].T, a["attn_Wbeta"].T, a["ffn_Wr"],
                                      router_bias, b1, tri], axis=1),
        "row_pack": np.concatenate([sel_half, sel_wd.astype(np.float32), sel_lr.astype(np.float32)], axis=1),
        "state_pack": np.stack([by_pairs(w_in0), by_pairs(w_out0), by_pairs(w_out0.transpose(0, 2, 1))], axis=1),
        "woT": a["attn_Wo"].T.reshape(pairs, 128, D).transpose(1, 0, 2),
    }
    nc = _bacc.Bacc("TRN2", target_bir_lowering=False, num_devices=1)
    given = {f"in_{k}": np.ascontiguousarray(v) for k, v in arrays.items()}
    aps = {k: nc.dram_tensor(f"in_{k}", given[f"in_{k}"].shape, _mybir.dt.from_np(given[f"in_{k}"].dtype),
                             kind="ExternalInput").ap() for k in arrays}
    aps["out"] = nc.dram_tensor("out", (B, L, D), _mybir.dt.float32, kind="ExternalOutput").ap()
    build(nc, **aps)
    r = _run(nc, [given], core_ids=[0])
    return r.results[0]["out"]
```
